# Optimizing a Trainium2 kernel written in Bass

```python
import numpy as np
import jax
import jax.numpy as jnp

def _softmax(x, axis=-1):
    return jax.nn.softmax(x, axis=axis)

def _gelu(x):
    return jax.nn.gelu(x, approximate=True)

def _silu(x):
    return jax.nn.silu(x)

def _sigmoid(x):
    return jax.nn.sigmoid(x)

def _layernorm(x, axis=-1, eps=1e-05):
    m = jnp.mean(x, axis=axis, keepdims=True)
    v = jnp.var(x, axis=axis, keepdims=True)
    return (x - m) / jnp.sqrt(v + eps)

def _scatter_add(tgt, idx, src, axis=0):
    return tgt.at[idx].add(src)

def _segment_sum(src, seg, n):
    return jax.ops.segment_sum(src, seg, n)
kernel_name = 'mk_prb_d2_jaxref_r8_d3ea71'

def setup_inputs(seed: int=0):
    np.random.seed(seed)
    _w = jnp.asarray

    def _L0_attn_setup():
        import jax, jax.numpy as jnp
        import numpy as np
        NUM_HEADS = 16
        LN_EPS = 1e-05
        FEAT_EPS = 0.0001
        key = jax.random.key(seed)
        ks = jax.random.split(key, 4)
        B, L, D = (2, 256, 128)
        scale = 0.02
        return {'x': jax.random.normal(ks[0], (B, L, D), dtype=jnp.float32), 'Wqkv': jax.random.normal(ks[1], (3 * D, D), dtype=jnp.float32) * scale, 'bqkv': jnp.zeros((3 * D,), dtype=jnp.float32), 'Wout': jax.random.normal(ks[2], (D, D), dtype=jnp.float32) * scale, 'bout': jnp.zeros((D,), dtype=jnp.float32), 'gamma': jnp.ones((D,), dtype=jnp.float32), 'beta': jnp.zeros((D,), dtype=jnp.float32)}
    _L0_attn_in = _L0_attn_setup()

    def _L0_ffn_setup():
        import jax, jax.numpy as jnp
        import numpy as np
        H = 128
        F = 512
        E = 8
        TOP_K = 2
        B, S = (1, 256)
        key = jax.random.key(seed)
        k0, k1, k2, k3 = jax.random.split(key, 4)
        hidden_states = jax.random.normal(k0, (B, S, H), dtype=jnp.float32)
        gate_w = jax.random.normal(k1, (E, H), dtype=jnp.float32) * 0.02
        gate_up_w = jax.random.normal(k2, (E, 2 * F, H), dtype=jnp.float32) * 0.02
        down_w = jax.random.normal(k3, (E, H, F), dtype=jnp.float32) * 0.02
        return {'hidden_states': hidden_states, 'gate_w': gate_w, 'gate_up_w': gate_up_w, 'down_w': down_w}
    _L0_ffn_in = _L0_ffn_setup()

    def _L1_attn_setup():
        import jax, jax.numpy as jnp
        import numpy as np
        from jax import lax
        L, B, S, D, H = (2, 8, 256, 128, 128)
        LOG_H0 = float(np.log(0.5))

        def _log_g(x):
            return jnp.where(x >= 0, jnp.log(jnp.where(x >= 0, x + 0.5, 1.0)), -jax.nn.softplus(-x))

        def _mingru_layer(x, Wz, bz, Wh, bh):
            k = jnp.einsum('bsd,hd->bsh', x, Wz) + bz
            log_z = -jax.nn.softplus(-k)
            log_coeffs = -jax.nn.softplus(k)
            pre_h = jnp.einsum('bsd,hd->bsh', x, Wh) + bh
            log_values = log_z + _log_g(pre_h)
            Bq = x.shape[0]
            log_coeffs = jnp.pad(log_coeffs, ((0, 0), (1, 0), (0, 0)))
            log_values = jnp.concatenate([jnp.full((Bq, 1, log_values.shape[-1]), LOG_H0, dtype=log_values.dtype), log_values], axis=1)
            a_star = jnp.cumsum(log_coeffs, axis=1)
            log_h = a_star + lax.cumlogsumexp(log_values - a_star, axis=1)
            return jnp.exp(log_h)[:, 1:]
        key = jax.random.key(seed)
        ks = jax.random.split(key, 5)
        stdv = 1.0 / np.sqrt(D)
        u = lambda k, shp: jax.random.uniform(k, shp, jnp.float32, -stdv, stdv)
        return {'x': jax.random.normal(ks[0], (B, S, D), jnp.float32), 'Wz': u(ks[1], (L, H, D)), 'bz': u(ks[2], (L, H)), 'Wh': u(ks[3], (L, H, D)), 'bh': u(ks[4], (L, H))}
    _L1_attn_in = _L1_attn_setup()

    def _L1_ffn_setup():
        import jax, jax.numpy as jnp
        import numpy as np
        EPS = 1e-12

        def _l2norm(v):
            n = jnp.sqrt(jnp.sum(v * v, axis=-1, keepdims=True))
            return v / jnp.maximum(n, EPS)
        key = jax.random.key(seed)
        ks = jax.random.split(key, 6)
        B, S, D, F, E = (2, 256, 128, 512, 8)
        std = 0.02
        return {'x': jax.random.normal(ks[0], (B, S, D), jnp.float32), 'Wp': jax.random.normal(ks[1], (D, D), jnp.float32) * (1.0 / np.sqrt(D)), 'sim_matrix': jax.random.normal(ks[2], (E, D), jnp.float32) * std, 'temperature': jnp.asarray(1.0, jnp.float32), 'W1': jax.random.normal(ks[3], (E, D, F), jnp.float32) * (1.0 / np.sqrt(D)), 'b1': jnp.zeros((E, F), jnp.float32), 'W2': jax.random.normal(ks[4], (E, F, D), jnp.float32) * (1.0 / np.sqrt(F)), 'b2': jnp.zeros((E, D), jnp.float32)}
    _L1_ffn_in = _L1_ffn_setup()
    _d = {'L0_attn_x': _L0_attn_in['x'], 'L0_attn_Wqkv': _L0_attn_in['Wqkv'], 'L0_attn_bqkv': _L0_attn_in['bqkv'], 'L0_attn_Wout': _L0_attn_in['Wout'], 'L0_attn_bout': _L0_attn_in['bout'], 'L0_attn_gamma': _L0_attn_in['gamma'], 'L0_attn_beta': _L0_attn_in['beta'], 'L0_ffn_gate_w': _L0_ffn_in['gate_w'], 'L0_ffn_gate_up_w': _L0_ffn_in['gate_up_w'], 'L0_ffn_down_w': _L0_ffn_in['down_w'], 'L1_attn_Wz': _L1_attn_in['Wz'], 'L1_attn_bz': _L1_attn_in['bz'], 'L1_attn_Wh': _L1_attn_in['Wh'], 'L1_attn_bh': _L1_attn_in['bh'], 'L1_ffn_Wp': _L1_ffn_in['Wp'], 'L1_ffn_sim_matrix': _L1_ffn_in['sim_matrix'], 'L1_ffn_temperature': _L1_ffn_in['temperature'], 'L1_ffn_W1': _L1_ffn_in['W1'], 'L1_ffn_b1': _L1_ffn_in['b1'], 'L1_ffn_W2': _L1_ffn_in['W2'], 'L1_ffn_b2': _L1_ffn_in['b2']}
    _x0 = _d['L0_attn_x']
    _d['L0_attn_x'] = jax.random.normal(jax.random.fold_in(jax.random.key(seed), 1), (8, 512, 128), dtype=_x0.dtype)
    del _x0
    return _d

def reference(L0_attn_x, L0_attn_Wqkv, L0_attn_bqkv, L0_attn_Wout, L0_attn_bout, L0_attn_gamma, L0_attn_beta, L0_ffn_gate_w, L0_ffn_gate_up_w, L0_ffn_down_w, L1_attn_Wz, L1_attn_bz, L1_attn_Wh, L1_attn_bh, L1_ffn_Wp, L1_ffn_sim_matrix, L1_ffn_temperature, L1_ffn_W1, L1_ffn_b1, L1_ffn_W2, L1_ffn_b2):

    def _L0_attn_ref(x, Wqkv, bqkv, Wout, bout, gamma, beta):
        import jax, jax.numpy as jnp
        import numpy as np
        NUM_HEADS = 16
        LN_EPS = 1e-05
        FEAT_EPS = 0.0001
        B, L, D = x.shape
        H = NUM_HEADS
        E = D // H
        qkv = x @ Wqkv.T + bqkv
        q, k, v = jnp.split(qkv, 3, axis=-1)
        q = q.reshape(B, L, H, E)
        k = k.reshape(B, L, H, E)
        v = v.reshape(B, L, H, E)
        q = (jax.nn.elu(q) + 1.0 + FEAT_EPS) / jnp.sqrt(jnp.asarray(E, q.dtype))
        k = jax.nn.elu(k) + 1.0 + FEAT_EPS
        kv = jnp.einsum('blhe,blhf->blhef', k, v)
        kv_cumsum = jnp.cumsum(kv, axis=1)
        k_cumsum = jnp.cumsum(k, axis=1)
        num = jnp.einsum('blhe,blhef->blhf', q, kv_cumsum)
        den = jnp.einsum('blhe,blhe->blh', q, k_cumsum)[..., None] + FEAT_EPS
        out = (num / den).reshape(B, L, D)
        out = out @ Wout.T + bout
        mu = jnp.mean(out, axis=-1, keepdims=True)
        var = jnp.var(out, axis=-1, keepdims=True)
        return (out - mu) / jnp.sqrt(var + LN_EPS) * gamma + beta

    def _L0_ffn_ref(hidden_states, gate_w, gate_up_w, down_w):
        import jax, jax.numpy as jnp
        import numpy as np
        H = 128
        F = 512
        E = 8
        TOP_K = 2
        B, S = (1, 256)
        b, s, h = hidden_states.shape
        x = hidden_states.reshape(-1, h)
        router_logits = x @ gate_w.T
        probs = jax.nn.softmax(router_logits.astype(jnp.float32), axis=-1)
        topw, sel = jax.lax.top_k(probs, TOP_K)
        topw = topw / jnp.sum(topw, axis=-1, keepdims=True)
        topw = topw.astype(x.dtype)
        combine = jnp.sum(jax.nn.one_hot(sel, E, dtype=x.dtype) * topw[..., None], axis=1)
        gu = jnp.einsum('th,efh->etf', x, gate_up_w)
        gate, up = (gu[..., :F], gu[..., F:])
        hact = up * jax.nn.gelu(gate, approximate=False)
        expert_out = jnp.einsum('etf,ehf->eth', hact, down_w)
        out = jnp.einsum('eth,te->th', expert_out, combine)
        return out.reshape(b, s, h)

    def _L1_attn_ref(x, Wz, bz, Wh, bh):
        import jax, jax.numpy as jnp
        import numpy as np
        from jax import lax
        L, B, S, D, H = (2, 8, 256, 128, 128)
        LOG_H0 = float(np.log(0.5))

        def _log_g(x):
            return jnp.where(x >= 0, jnp.log(jnp.where(x >= 0, x + 0.5, 1.0)), -jax.nn.softplus(-x))

        def _mingru_layer(x, Wz, bz, Wh, bh):
            k = jnp.einsum('bsd,hd->bsh', x, Wz) + bz
            log_z = -jax.nn.softplus(-k)
            log_coeffs = -jax.nn.softplus(k)
            pre_h = jnp.einsum('bsd,hd->bsh', x, Wh) + bh
            log_values = log_z + _log_g(pre_h)
            Bq = x.shape[0]
            log_coeffs = jnp.pad(log_coeffs, ((0, 0), (1, 0), (0, 0)))
            log_values = jnp.concatenate([jnp.full((Bq, 1, log_values.shape[-1]), LOG_H0, dtype=log_values.dtype), log_values], axis=1)
            a_star = jnp.cumsum(log_coeffs, axis=1)
            log_h = a_star + lax.cumlogsumexp(log_values - a_star, axis=1)
            return jnp.exp(log_h)[:, 1:]
        h = x
        for l in range(Wz.shape[0]):
            h = _mingru_layer(h, Wz[l], bz[l], Wh[l], bh[l])
        return h

    def _L1_ffn_ref(x, Wp, sim_matrix, temperature, W1, b1, W2, b2):
        import jax, jax.numpy as jnp
        import numpy as np
        EPS = 1e-12

        def _l2norm(v):
            n = jnp.sqrt(jnp.sum(v * v, axis=-1, keepdims=True))
            return v / jnp.maximum(n, EPS)
        E = sim_matrix.shape[0]
        top_k = 2
        proj = jnp.einsum('bsd,ed->bse', x, Wp)
        pn = _l2norm(proj)
        sn = _l2norm(sim_matrix)
        gate_scores = jnp.einsum('bsd,ed->bse', pn, sn) / temperature
        top_v, top_i = jax.lax.top_k(gate_scores, top_k)
        gate_probs = jax.nn.softmax(top_v, axis=-1)
        comb = jnp.sum(jax.nn.one_hot(top_i, E, dtype=x.dtype) * gate_probs[..., None], axis=-2)
        h = jax.nn.gelu(jnp.einsum('bsd,edf->ebsf', x, W1) + b1[:, None, None, :], approximate=False)
        eo = jnp.einsum('ebsf,efd->ebsd', h, W2) + b2[:, None, None, :]
        out = jnp.einsum('ebsd,bse->bsd', eo, comb)
        return out
    x = L0_attn_x
    xn = _layernorm(x, axis=-1)
    x = x + _L0_attn_ref(xn, L0_attn_Wqkv, L0_attn_bqkv, L0_attn_Wout, L0_attn_bout, L0_attn_gamma, L0_attn_beta) + _L0_ffn_ref(xn, L0_ffn_gate_w, L0_ffn_gate_up_w, L0_ffn_down_w)
    xn = _layernorm(x, axis=-1)
    x = x + _L1_attn_ref(xn, L1_attn_Wz, L1_attn_bz, L1_attn_Wh, L1_attn_bh) + _L1_ffn_ref(xn, L1_ffn_Wp, L1_ffn_sim_matrix, L1_ffn_temperature, L1_ffn_W1, L1_ffn_b1, L1_ffn_W2, L1_ffn_b2)
    return x

_drawn_inputs = setup_inputs


def setup_inputs(seed=0):
    import zlib

    import numpy as np

    out = dict(_drawn_inputs(seed))
    spreads = {'L0_attn_bqkv': (0.0, 0.1),
     'L0_attn_bout': (0.0, 0.1),
     'L0_attn_gamma': (1.0, 0.2),
     'L0_attn_beta': (0.0, 0.1),
     'L1_ffn_b1': (0.0, 0.284),
     'L1_ffn_b2': (0.0, 0.1)}
    factors = {'L0_ffn_gate_w': 3.692,
     'L0_ffn_gate_up_w': 3.408,
     'L0_ffn_down_w': 3.741,
     'L1_attn_Wz': 6.576,
     'L1_attn_bz': 64.0,
     'L1_attn_bh': 2.746}
    for name, (base, spread) in spreads.items():
        noise = np.random.default_rng([zlib.crc32(name.encode()), seed]).standard_normal(out[name].shape)
        drawn = base * np.exp(spread * noise) if base else spread * noise
        out[name] = jnp.asarray(drawn.astype(out[name].dtype))
    for name, factor in factors.items():
        out[name] = (out[name] * factor).astype(out[name].dtype)
    return out
```

```python
import concourse.bass as bass
from concourse import mybir
from concourse.alu_op_type import AluOpType as ALU
from contextlib import ExitStack

P = 128
B, S, D = 8, 512, 128
NT = B * S // P
TPS = S // P
H, HE = 16, 8
E, F = 8, 512
FC = F // P
NBLK = 2 * NT + E
FEAT_EPS = 1e-4
LN_EPS = 1e-5
NORM_EPS = 1e-12
LOADS = 4
TPL = NT // LOADS
BIG = 3.0e38


class Chain:

    def __init__(self, engine, sem):
        self.engine, self.sem, self.before, self.n, self.base = engine, sem, 0, 0, None

    def enter(self, i, steps):
        self.before += self.n
        self.base, self.steps, self.n = i * steps + self.before, steps, 0

    def leave(self, rounds):
        assert self.n == self.steps, (self.n, self.steps)
        self.before, self.base, self.n = self.before + self.steps * rounds, None, 0

    def add(self, ins):
        ins.then_inc(self.sem, 1)
        self.n += 1

    def wait(self):
        self.engine.wait_ge(self.sem, self.n + (self.before if self.base is None else self.base))

    def link(self, ins):
        self.add(ins)
        self.wait()


def build(nc, x_d, wqkv_d, bqk_d, bv_d, wout_d, bout_d, gamma_d, beta_d, gatew_d, gu_d, dw_d,
          wz_d, bz_d, wh_d, bh_d, wp_d, sim_d, temp_d, w1_d, b1_d, w2_d, b2_d, xg_d, yg_d, out_d):
    fp32, bf16 = mybir.dt.float32, mybir.dt.bfloat16
    i32, u32 = mybir.dt.int32, mybir.dt.uint32
    ACT = mybir.ActivationFunctionType
    AX = mybir.AxisListType

    ctx = ExitStack()
    with ctx:
        def sb(name, shape, dt=fp32):
            return ctx.enter_context(nc.sbuf_tensor(name, shape, dt))

        def sem(name):
            return ctx.enter_context(nc.semaphore(name))

        def sem2(name):
            return [sem(name + "_even"), sem(name + "_odd")]

        x = sb("x", [P, NT * D])
        xn = sb("xn", [P, NT * D])
        xnT = sb("xnT", [P, NT * P])
        attn_o = xnT
        gu = sb("gu", [P, E * 2 * F])
        dw = sb("dw", [P, E * FC * D])
        y1 = gu[:, 0:NT * D]
        y2 = gu[:, NT * D:2 * NT * D]
        big = sb("big", [P, 12288])
        w1 = big[:, 0:E * F]
        w2 = big[:, E * F:2 * E * F]
        b1b = big[:, 2 * E * F:3 * E * F]
        b2b = sb("b2b", [P, E * D])
        qx = [big[:, 2048 * s:2048 * (s + 1)] for s in range(2)]
        vpad = [big[:, 4096 + 2048 * s:4096 + 2048 * (s + 1)] for s in range(2)]
        am = [big[:, 8192 + 2048 * s:8192 + 2048 * (s + 1)] for s in range(2)]
        xT_ring = [sb(f"xT_ring{s}", [P, S]) for s in range(2)]
        scr = [[sb(f"scr{s}_{k}", [P, S]) for k in range(6)] for s in range(2)]
        kcum = sb("kcum", [P, S])
        prod = sb("prod", [P, S])
        dens = sb("dens", [P, S])
        rden = sb("rden", [P, S])
        done_mark = sb("done_mark", [1, 1])
        ident = sb("ident", [P, P])
        ones = sb("ones", [P, S])
        tri = sb("tri", [P, P])
        headblk = sb("headblk", [P, P])
        headblk_q = sb("headblk_q", [P, P])
        jmask = sb("jmask", [P, 4])
        upper16 = sb("upper16", [P, P], bf16)
        ones16 = sb("ones16", [P, P], bf16)
        zero = sb("zero", [P, D])
        rev = sb("rev", [P, E])
        blk_start = sb("blk_start", [1, NBLK])
        wqkv = sb("wqkv", [P, 3 * D])
        wout = sb("wout", [P, D])
        gatew = sb("gatew", [P, E])
        wz = sb("wz", [P, 2 * D])
        wh = sb("wh", [P, 2 * D])
        wp = sb("wp", [P, D])
        bqk = sb("bqk", [P, 2])
        bqke = sb("bqke", [P, 2])
        bzh = sb("bzh", [P, 4])
        bzh2 = sb("bzh2", [P, 4])
        bvb = sb("bvb", [P, D])
        boutb = sb("boutb", [P, D])
        gammab = sb("gammab", [P, D])
        betab = sb("betab", [P, D])
        tempb = sb("tempb", [P, 1])
        rtemp = sb("rtemp", [P, 1])
        sim = sb("sim", [E, D])
        simsq = kcum[0:E, 0:D]
        simn = sb("simn", [E, 4])
        simT = sb("simT", [P, E])
        half8 = sb("half8", [E, 1])
        state = [sb(f"state{s}", [P, P]) for s in range(2)]
        st = sb("st", [P, NT * 6])
        sto_cmp = sb("sto_cmp", [P, NBLK * E])
        sto = sto_cmp[:, 0:NT * 6]
        ln = sb("ln", [P, 6 * NT])
        lno = sb("lno", [P, 6 * NT])
        neghalf = sb("neghalf", [P, NT])
        lg = sb("lg", [P, NT * E])
        rt = [a[:, k * NT * E:(k + 1) * NT * E] for a in (kcum, prod, dens, rden) for k in range(2)]
        rs = [sb(f"rs{k}", [P, NT]) for k in range(8)]
        r9 = sb("r9", [P, E + 1])
        r8 = [sb(f"r8_{k}", [P, E]) for k in range(5)]
        r8i = [sb(f"r8i_{k}", [P, E], i32) for k in range(2)]
        m16 = sb("m16", [P, NT * E], bf16)
        wgt = [[sb(f"wgt{l}_{k}", [P, NT]) for k in range(2)] for l in range(2)]
        dst = [[sb(f"dst{l}_{k}", [P, NT], u32) for k in range(2)] for l in range(2)]
        cmpb = sto_cmp[0:1, 0:NBLK * E]
        bexf = sb("bexf", [1, NBLK])
        bex = [sb(f"bex{l}", [1, NBLK], i32) for l in range(2)]
        eq, ek, rq, rk, ktok, attnT = ([scr[s][k] for s in range(2)] for k in range(6))
        qT, kT = rq, rk
        ga, gz, gs, gh1, gh2 = ([scr[s][k] for s in range(2)] for k in range(5))
        sq = ga
        projT = gz
        fa, fh, hT = ([scr[s][k] for s in range(2)] for k in range(3))
        xg, xgT, yb = ([scr[s][3][:, k * P:(k + 1) * P] for s in range(2)] for k in range(3))
        xn_ring = [scr[s][5] for s in range(2)]

        bank = [ctx.enter_context(nc.psum_tensor(f"bank{k}", [P, 512], fp32)) for k in range(8)]

        x_in = [sem(f"x_in{k}") for k in range(LOADS)]
        small_in = sem("small_in")
        gu_in = sem("gu_in")
        dw_in = sem("dw_in")
        w2_in = sem("w2_in")
        xg_zeroed = sem("xg_zeroed")
        pool_step = sem("pool_step")
        consts_ready = sem("consts_ready")
        zero_ready = sem("zero_ready")
        dve_step = sem("dve_step")
        act_step = sem("act_step")
        var_ready = [sem(f"var_ready{k}") for k in range(2)]
        rstd_ready = [sem(f"rstd_ready{k}") for k in range(2)]
        xn_ready = [sem2(f"xn_ready{k}") for k in range(2)]
        xn_kept = [sem2(f"xn_kept{k}") for k in range(2)]
        xT_psum = [sem2(f"xT_psum{k}") for k in range(2)]
        xT_ready = [sem2(f"xT_ready{k}") for k in range(2)]
        scored = [sem2(f"scored{k}") for k in range(2)]
        proj_psum, proj_ready = sem2("proj_psum"), sem2("proj_ready")
        gap_ready = [sem(f"gap_ready{k}") for k in range(2)]
        gap_exp = [sem(f"gap_exp{k}") for k in range(2)]
        picks_ready = [sem(f"picks_ready{k}") for k in range(2)]
        ranks_psum = [sem(f"ranks_psum{k}") for k in range(2)]
        dest_ready = [sem(f"dest_ready{k}") for k in range(2)]
        scattered = [sem(f"scattered{k}") for k in range(2)]
        simn_ready, simT_psum, simT_ready = sem("simn_ready"), sem("simT_psum"), sem("simT_ready")
        sim_sq, sim_pow = sem("sim_sq"), sem("sim_pow")
        vpad_zeroed = sem("vpad_zeroed")
        xv_in = sem2("xv_in")
        q_psum, k_psum, qk_read, qk_exp = sem("q_psum"), sem("k_psum"), sem("qk_read"), sem("qk_exp")
        v_psum, v_ready, kt_psum, kt_ready = sem("v_psum"), sem("v_ready"), sem("kt_psum"), sem("kt_ready")
        q_ready, k_ready, prod_ready, qx_ready = sem("q_ready"), sem("k_ready"), sem("prod_ready"), sem("qx_ready")
        den_psum, den_read = sem("den_psum"), sem("den_read")
        score_psum = sem("score_psum")
        am_ready = sem("am_ready")
        kv_psum, state_ready = sem("kv_psum"), sem("state_ready")
        num_psum, attn_ready = sem("num_psum"), sem("attn_ready")
        o_psum, o_ready = sem("o_psum"), sem("o_ready")
        varo_ready = sem("varo_ready")
        stats_done = sem("stats_done")
        norm_ready, norm_pow = sem("norm_ready"), sem("norm_pow")
        attn_added = sem("attn_added")
        m = {n: sem2(n) for n in (
            "xg_in", "xgT_psum", "xgT_ready", "gate_psum", "up_psum", "act_ready", "pre_ready", "h_ready",
            "hT_psum", "hT_ready", "y_psum", "y_ready", "y_out")}
        gathered = [[sem(f"gathered{l}_{k}") for k in range(LOADS)] for l in range(2)]
        gru_psum = [sem2(f"gru_psum{l}") for l in range(2)]
        gru_act = [sem2(f"gru_act{l}") for l in range(2)]
        gru_scan = [sem2(f"gru_scan{l}") for l in range(2)]
        gruT_psum, gruT_added = sem2("gruT_psum"), sem2("gruT_added")
        out_ready = [sem(f"out_ready{k}") for k in range(LOADS)]
        stored = sem("stored")

        block = ctx.enter_context(nc.Block())

        SMALL = [(wqkv, wqkv_d), (wout, wout_d), (gatew, gatew_d), (wz, wz_d), (wh, wh_d), (wp, wp_d),
                 (bqk, bqk_d), (bzh[:, 0:2], bz_d), (bzh[:, 2:4], bh_d), (sim, sim_d)]
        BCAST = [(bvb, bv_d), (boutb, bout_d), (gammab, gamma_d), (betab, beta_d), (tempb, temp_d), (b2b, b2_d)]
        NSMALL = 16 * (len(SMALL) + len(BCAST))
        x_rows = x_d.rearrange("b (c p) d -> p (b c) d", p=P)
        out_rows = out_d.rearrange("b (c p) d -> p (b c) d", p=P)

        def diag(vt):
            v = vt.rearrange("p (g r c) -> p g r c", g=4, r=4)[:, :, :, 0:HE]
            pairs = [list(a) for a in v.ap]
            assert pairs[2][0] == 32, pairs
            pairs[2][0] = 40
            return bass.AP(v.tensor, v.offset, pairs)

        @block.sync
        def _(sp):
            for k in range(LOADS):
                sp.dma_start(x[:, k * TPL * D:(k + 1) * TPL * D].rearrange("p (t d) -> p t d", d=D),
                             x_rows[:, k * TPL:(k + 1) * TPL, :]).then_inc(x_in[k], 16)
            for to, src in SMALL:
                sp.dma_start(to[:] if to is not bzh else to, src).then_inc(small_in, 16)
            for to, src in BCAST:
                sp.dma_start(to[:], src.partition_broadcast(P)).then_inc(small_in, 16)
            sp.wait_ge(zero_ready, 1)
            sp.dma_start(xg_d.rearrange("(c p) d -> p c d", p=P),
                         zero[:].unsqueeze(1).to_broadcast([P, NBLK, D])).then_inc(xg_zeroed, 16)
            sp.dma_start(gu[:], gu_d).then_inc(gu_in, 16)
            sp.dma_start(dw[:], dw_d).then_inc(dw_in, 16)

            def keep_xn(l):
                with sp.Fori(0, B // 2) as i:
                    for s in range(2):
                        sp.wait_ge(xn_ready[l][s], i * TPS + TPS)
                        sp.dma_start(xn[:, bass.ds(i * 2 * S + s * S, S)], xn_ring[s][:]).then_inc(xn_kept[l][s], 16)

            keep_xn(0)
            with sp.Fori(0, B // 2) as i:
                for s in range(2):
                    sp.wait_ge(scored[0][s], B // 2)
                    sp.wait_ge(v_psum, i * 2 + (s - 1 if s else 0))
                    sp.dma_start(xT_ring[s][:], xnT[:, bass.ds(i * 2 * S + s * S, S)]).then_inc(xv_in[s], 16)

            def load_blocks(l):
                o = l * NBLK // 2
                sp.wait_ge(scattered[l], 16 * 2 * NT)
                with sp.Fori(0, NBLK // 2) as i:
                    for s in range(2):
                        sp.wait_ge(m["xgT_psum"][s], i + o)
                        sp.dma_start(xg[s][:], xg_d[bass.ds(i * 2 * P + s * P, P), :]).then_inc(m["xg_in"][s], 16)

            sp.wait_ge(o_ready, B)
            sp.dma_start(w1, w1_d).then_inc(w2_in, 16)
            sp.dma_start(w2, w2_d).then_inc(w2_in, 16)
            sp.dma_start(b1b, b1_d.partition_broadcast(P)).then_inc(w2_in, 16)
            load_blocks(0)
            keep_xn(1)
            for s in range(2):
                sp.wait_ge(gruT_added[s], B // 2)
            load_blocks(1)
            for k in range(LOADS):
                sp.wait_ge(out_ready[k], 1)
                sp.dma_start(out_rows[:, k * TPL:(k + 1) * TPL, :],
                             x[:, k * TPL * D:(k + 1) * TPL * D].rearrange("p (t d) -> p t d", d=D)).then_inc(stored, 16)
            sp.wait_ge(stored, 16 * LOADS)

        @block.gpsimd
        def _(pool):
            c = Chain(pool, pool_step)
            pool.memset(zero[:], 0.0).then_inc(zero_ready, 1)
            for to, v in ((ident, 0.0), (ones, 1.0), (tri, 1.0), (headblk, 1.0), (headblk_q, HE ** -0.5),
                          (jmask, HE ** -0.5), (upper16, 1.0), (ones16, 1.0), (neghalf, -0.5), (half8, -0.5)):
                c.add(pool.memset(to[:], v))
            c.wait()

            def select(t, pattern, base, mult, op, fill):
                c.add(pool.affine_select(out=t, in_=t, compare_op=op, fill=fill, base=base, pattern=pattern,
                                         channel_multiplier=mult))

            select(ident[:], [[-1, P]], 0, 1, ALU.not_equal, 1.0)
            select(tri[:], [[1, P]], 0, -1, ALU.is_ge, 0.0)
            select(upper16[:], [[1, P]], -1, -1, ALU.is_ge, 0.0)
            for t in (headblk, headblk_q):
                v = t[:].rearrange("p (h c) -> p h c", c=HE)
                select(v, [[-HE, H], [0, HE]], 0, 1, ALU.is_ge, 0.0)
                c.wait()
                select(v, [[HE, H], [0, HE]], HE - 1, -1, ALU.is_ge, 0.0)
            c.add(pool.iota(blk_start[:], [[P, NBLK]], base=0, channel_multiplier=0, allow_small_or_imprecise_dtypes=True))
            c.add(pool.iota(rev[:], [[-1, E]], base=E, channel_multiplier=0, allow_small_or_imprecise_dtypes=True))
            c.wait()
            jv = headblk_q[:].rearrange("p (g j c) -> p j g c", g=4, j=4)
            c.link(pool.tensor_tensor(out=jmask[:], in0=jv[:, :, 0, 0], in1=jv[:, :, 1, 0], op=ALU.add))
            c.link(pool.tensor_tensor(out=jmask[:], in0=jmask[:], in1=jv[:, :, 2, 0], op=ALU.add))
            pool.tensor_tensor(out=jmask[:], in0=jmask[:], in1=jv[:, :, 3, 0], op=ALU.add).then_inc(consts_ready, 1)
            for s in range(2):
                pool.memset(vpad[s], 0.0).then_inc(vpad_zeroed, 1)
            pool.wait_ge(sim_sq, 1)
            pool.tensor_tensor(out=simn[:, 1:2], in0=simn[:, 0:1], in1=half8[:], op=ALU.pow).then_inc(sim_pow, 1)

            def rstd(l):
                pool.wait_ge(var_ready[l], 1)
                pool.tensor_tensor(out=ln[:, NT:2 * NT], in0=ln[:, 2 * NT:3 * NT], in1=neghalf[:], op=ALU.pow)\
                    .then_inc(rstd_ready[l], 1)

            def scatter(l):
                pool.wait_ge(dest_ready[l], 1)
                for s in range(2):
                    pool.wait_ge(xn_kept[l][s], 16 * B // 2)
                if l == 0:
                    pool.wait_ge(xg_zeroed, 16)
                for t in range(NT):
                    for k in range(2):
                        pool.indirect_dma_start(xg_d, bass.IndirectOffsetOnAxis(ap=dst[l][k][:, t:t + 1], axis=0),
                                                xn[:, t * D:(t + 1) * D], None).then_inc(scattered[l], 16)

            def gather(l):
                for s in range(2):
                    pool.wait_ge(m["y_out"][s], 16 * (NBLK // 2) * (l + 1))
                for t in range(NT):
                    for k, y in enumerate((y1, y2)):
                        pool.indirect_dma_start(y[:, t * D:(t + 1) * D], None, yg_d,
                                                bass.IndirectOffsetOnAxis(ap=dst[l][k][:, t:t + 1], axis=0))\
                            .then_inc(gathered[l][t // TPL], 16)

            rstd(0)
            scatter(0)
            pool.wait_ge(varo_ready, 1)

            def tiles(a):
                return a.rearrange("p (t d) -> p t d", d=D)

            def per_tile(a):
                return a.unsqueeze(2).to_broadcast([P, NT, D])

            def per_channel(a):
                return a.unsqueeze(1).to_broadcast([P, NT, D])

            c.link(pool.tensor_tensor(out=lno[:, NT:2 * NT], in0=lno[:, 2 * NT:3 * NT], in1=neghalf[:], op=ALU.pow))
            o = tiles(attn_o[:])
            c.link(pool.tensor_tensor(out=o, in0=o, in1=per_tile(lno[:, 0:NT]), op=ALU.subtract))
            c.link(pool.tensor_tensor(out=o, in0=o, in1=per_tile(lno[:, NT:2 * NT]), op=ALU.mult))
            c.link(pool.tensor_tensor(out=o, in0=o, in1=per_channel(gammab[:]), op=ALU.mult))
            c.link(pool.tensor_tensor(out=o, in0=o, in1=per_channel(betab[:]), op=ALU.add))
            pool.tensor_tensor(out=x[:], in0=x[:], in1=attn_o[:], op=ALU.add).then_inc(attn_added, 1)
            gather(0)
            rstd(1)
            pool.wait_ge(norm_ready, 1)
            pool.tensor_tensor(out=rs[2][:], in0=rs[1][:], in1=neghalf[:], op=ALU.pow).then_inc(norm_pow, 1)
            scatter(1)
            gather(1)

        @block.tensor
        def _(pe):
            mm = nc.tensor.matmul
            pe.wait_ge(consts_ready, 1)
            pe.wait_ge(small_in, NSMALL)
            pe.wait_ge(simn_ready, 1)
            nc.tensor.transpose(bank[7][:, 0:E], sim[:], ident[0:E, 0:E]).then_inc(simT_psum, 1)
            pe.wait_ge(simT_ready, 1)

            with pe.Fori(0, B // 2) as i:
                for s in range(2):
                    pe.wait_ge(xn_ready[0][s], i * TPS + TPS)
                    pe.wait_ge(xT_ready[0][s], i)
                    for j in range(TPS):
                        ins = nc.tensor.transpose(bank[s][:, j * P:(j + 1) * P], xn_ring[s][:, j * D:(j + 1) * D],
                                                  ident[:])
                    ins.then_inc(xT_psum[0][s], 1)
                for s in range(2):
                    pe.wait_ge(xT_ready[0][s], i + 1)
                    for j in range(TPS):
                        ins = mm(bank[4][:, bass.ds(i * 2 * TPS * E + (s * TPS + j) * E, E)],
                                 xT_ring[s][:, j * P:(j + 1) * P], gatew[:], start=True, stop=True)
                    ins.then_inc(scored[0][s], 1)

            def ranks(l):
                pe.wait_ge(picks_ready[l], 1)
                mm(bank[5][:, 0:256], upper16[:], m16[:], start=True, stop=True)
                mm(bank[5][:, 256:512], ones16[:], m16[:], start=True, stop=True).then_inc(ranks_psum[l], 1)

            ranks(0)

            with pe.Fori(0, B // 2) as i:
                for s in range(2):
                    q = i * 2 + s
                    tok = bass.ds(i * 2 * S + s * S, S)
                    if s == 0:
                        pe.wait_ge(gap_ready[0], 1)
                        pe.wait_ge(dest_ready[0], 1)
                    pe.wait_ge(den_read, q)
                    mm(bank[6][:], wqkv[:, 0:D], xnT[:, tok], start=True, stop=True).then_inc(q_psum, 1)
                    pe.wait_ge(o_ready, q)
                    mm(bank[7][:], wqkv[:, D:2 * D], xnT[:, tok], start=True, stop=True).then_inc(k_psum, 1)
                    pe.wait_ge(xv_in[s], i * 16 + 16)
                    pe.wait_ge(q_ready, q + 1)
                    for j in range(TPS):
                        ins = mm(bank[6][:, j * P:(j + 1) * P], xT_ring[s][:, j * P:(j + 1) * P],
                                 wqkv[:, 2 * D:3 * D], start=True, stop=True)
                    ins.then_inc(v_psum, 1)
                    pe.wait_ge(k_ready, q + 1)
                    for j in range(TPS):
                        ins = nc.tensor.transpose(bank[7][:, j * P:(j + 1) * P], kT[s][:, j * P:(j + 1) * P], ident[:])
                    ins.then_inc(kt_psum, 1)
                    pe.wait_ge(prod_ready, q + 1)
                    pe.wait_ge(v_ready, q * TPS + TPS)
                    mm(bank[6][:], headblk[:], prod[:], start=True, stop=True).then_inc(den_psum, 1)
                    pe.wait_ge(kt_ready, q + 1)
                    pe.wait_ge(qx_ready, q + 1)
                    for j in range(TPS):
                        for g in range(4):
                            pe.wait_ge(am_ready, q * 16 + (4 * j + g - 3 if j else 0))
                            mm(bank[g][:], kT[s][32 * g:32 * g + 32, j * P:(j + 1) * P],
                               qx[s].rearrange("p (t c) -> p t c", t=TPS)[32 * g:32 * g + 32, j, :],
                               start=True, stop=True).then_inc(score_psum, 1)
                        vt = vpad[s].rearrange("p (t n) -> p t n", t=TPS)[:, j, :]
                        cols = slice(j * P, (j + 1) * P)
                        pe.wait_ge(state_ready, q * (TPS - 1) + j)
                        if j < TPS - 1:
                            mm(bank[5][:, 0:P].rearrange("p (g r c) -> p g r c", g=4, r=4), ktok[s][:, cols],
                               diag(vt), start=(j == 0), stop=True, skip_group_check=True).then_inc(kv_psum, 1)
                        if j == 0:
                            pe.wait_ge(attn_ready, q)
                        else:
                            mm(bank[4][:, cols], state[(j - 1) % 2][:], qT[s][:, cols], start=True, stop=False,
                               skip_group_check=True)
                        for g in range(4):
                            pe.wait_ge(am_ready, q * 16 + 4 * j + g + 1)
                            for r in range(4):
                                h = 4 * g + r
                                ins = mm(bank[4][32 * g:32 * g + 32, cols], vt[:, 32 * h:32 * h + 32],
                                         am[j % 2][:, (4 * g + r) * P:(4 * g + r + 1) * P],
                                         start=(j == 0 and r == 0), stop=(r == 3), skip_group_check=True)
                        ins.then_inc(num_psum, 1)
                    pe.wait_ge(attn_ready, q + 1)
                    for j in range(TPS):
                        ins = mm(bank[7][:, j * P:(j + 1) * P], attnT[s][:, j * P:(j + 1) * P], wout[:],
                                 start=True, stop=True)
                    ins.then_inc(o_psum, 1)

            def ffn(l):
                o = l * NBLK // 2
                psx, psy, psh = bank[6], bank[7], bank[5]
                psg, psu = [bank[0], bank[1]], [bank[2], bank[3]]
                wa, wb, wid = (gu, dw[:], 2 * F) if l == 0 else (w1, w2, F)

                def xpose(s, n):
                    pe.wait_ge(m["xg_in"][s], (n + o) * 16 + 16)
                    pe.wait_ge(m["xgT_ready"][1 - s], n + s + o)
                    nc.tensor.transpose(psx[:, s * P:(s + 1) * P], xg[s][:], ident[:]).then_inc(m["xgT_psum"][s], 1)

                def up(s, n):
                    e = pe.value_load(bex[l][0:1, bass.ds(2 * n + s, 1)], min_val=0, max_val=E - 1)
                    pe.wait_ge(m["xgT_ready"][s], n + 1 + o)
                    pe.wait_ge(m["act_ready" if l == 0 else "pre_ready"][s], n)
                    mm(psg[s][:], xgT[s][:], wa[:, bass.ds(e * wid, F)], start=True, stop=True)\
                        .then_inc(m["gate_psum"][s], 1)
                    if l == 0:
                        pe.wait_ge(m["h_ready"][s], n + o)
                        mm(psu[s][:], xgT[s][:], wa[:, bass.ds(e * wid + F, F)], start=True, stop=True)\
                            .then_inc(m["up_psum"][s], 1)

                def down(s, n):
                    e = pe.value_load(bex[l][0:1, bass.ds(2 * n + s, 1)], min_val=0, max_val=E - 1)
                    pe.wait_ge(m["hT_ready"][s], n + 1 + o)
                    pe.wait_ge(m["y_ready"][1 - s], n + s + o)
                    for fc in range(FC):
                        ins = mm(psy[:, s * P:(s + 1) * P], hT[s][:, fc * P:(fc + 1) * P],
                                 wb[:, bass.ds(e * FC * D + fc * D, D)], start=(fc == 0), stop=(fc == FC - 1))
                    ins.then_inc(m["y_psum"][s], 1)

                def xpose_h(s, n):
                    hidden = fh
                    pe.wait_ge(m["h_ready"][s], n + 1 + o)
                    pe.wait_ge(m["hT_ready"][1 - s], n + s + o)
                    for fc in range(FC):
                        ins = nc.tensor.transpose(psh[:, fc * P:(fc + 1) * P], hidden[s][:, fc * P:(fc + 1) * P], ident[:])
                    ins.then_inc(m["hT_psum"][s], 1)

                xpose(0, 0)
                xpose(1, 0)
                up(0, 0)
                xpose(0, 1)
                up(1, 0)
                xpose_h(0, 0)
                with pe.Fori(0, NBLK // 2 - 2) as i:
                    xpose(1, i + 1)
                    up(0, i + 1)
                    down(0, i)
                    xpose_h(1, i)
                    xpose(0, i + 2)
                    up(1, i + 1)
                    down(1, i)
                    xpose_h(0, i + 1)
                n = NBLK // 2 - 1
                xpose(1, n)
                up(0, n)
                down(0, n - 1)
                xpose_h(1, n - 1)
                up(1, n)
                down(1, n - 1)
                xpose_h(0, n)
                down(0, n)
                xpose_h(1, n)
                down(1, n)

            pe.wait_ge(gu_in, 16)
            pe.wait_ge(dw_in, 16)
            pe.wait_ge(o_ready, B)
            ffn(0)

            with pe.Fori(0, B // 2) as i:
                for s in range(2):
                    pe.wait_ge(xn_ready[1][s], i * TPS + TPS)
                    pe.wait_ge(xT_ready[1][s], i)
                    for j in range(TPS):
                        ins = nc.tensor.transpose(bank[s][:, j * P:(j + 1) * P], xn_ring[s][:, j * D:(j + 1) * D],
                                                  ident[:])
                    ins.then_inc(xT_psum[1][s], 1)
                for s in range(2):
                    pe.wait_ge(xT_ready[1][s], i + 1)
                    pe.wait_ge(proj_ready[s], i)
                    mm(bank[2 + s][:], wp[:], xT_ring[s][:], start=True, stop=True).then_inc(proj_psum[s], 1)
                for s in range(2):
                    pe.wait_ge(proj_ready[s], i + 1)
                    for j in range(TPS):
                        cols = slice(j * P, (j + 1) * P)
                        mm(bank[4][:, bass.ds(i * 2 * TPS * E + (s * TPS + j) * E, E)], projT[s][:, cols], simT[:],
                           start=True, stop=True)
                        ins = mm(bank[6][:, bass.ds(i * 2 * TPS + s * TPS + j, 1)], sq[s][:, cols], ones[:, 0:1],
                                 start=True, stop=True)
                    ins.then_inc(scored[1][s], 1)
            ranks(1)

            with pe.Fori(0, B // 2) as i:
                for l in range(2):
                    for s in range(2):
                        pe.wait_ge(gru_scan[1 - l][s], i + l)
                        rhs = xnT[:, bass.ds(i * 2 * S + s * S, S)] if l == 0 else gh1[s][:]
                        mm(bank[2 * s][:], wz[:, l * D:(l + 1) * D], rhs, start=True, stop=True)
                        mm(bank[2 * s + 1][:], wh[:, l * D:(l + 1) * D], rhs, start=True, stop=True)\
                            .then_inc(gru_psum[l][s], 1)
                for s in range(2):
                    pe.wait_ge(gru_scan[1][s], i + 1)
                    pe.wait_ge(gruT_added[s], i)
                    if s == 0:
                        pe.wait_ge(dest_ready[1], 1)
                    for j in range(TPS):
                        ins = nc.tensor.transpose(bank[6 + s][:, j * P:(j + 1) * P], gh2[s][:, j * P:(j + 1) * P],
                                                  ident[:])
                    ins.then_inc(gruT_psum[s], 1)
            pe.wait_ge(w2_in, 48)
            for s in range(2):
                pe.wait_ge(gruT_added[s], B // 2)
            ffn(1)

        @block.scalar
        def _(act):
            fn = nc.scalar.activation

            def evict_xT(l):
                with act.Fori(0, B // 2) as i:
                    for s in range(2):
                        act.wait_ge(xT_psum[l][s], i + 1)
                        act.wait_ge(scored[l][s], i)
                        fn(xnT[:, bass.ds(i * 2 * S + s * S, S)], bank[s][:], ACT.Copy)
                        fn(xT_ring[s][:], bank[s][:], ACT.Copy).then_inc(xT_ready[l][s], 1)
                    if l == 1:
                        for s in range(2):
                            act.wait_ge(proj_psum[s], i + 1)
                            fn(projT[s][:], bank[2 + s][:], ACT.Copy)
                            fn(sq[s][:], bank[2 + s][:], ACT.Square).then_inc(proj_ready[s], 1)

            def gap_exps(l):
                act.wait_ge(gap_ready[l], 1)
                fn(rs[5][:], rs[4][:], ACT.Exp).then_inc(gap_exp[l], 1)

            evict_xT(0)
            gap_exps(0)
            with act.Fori(0, B // 2) as i:
                for s in range(2):
                    q = i * 2 + s
                    act.wait_ge(q_psum, q + 1)
                    act.wait_ge(prod_ready, q - s)
                    fn(eq[s][:], bank[6][:], ACT.Exp, bias=bqk[:, 0:1]).then_inc(qk_exp, 1)
                    act.wait_ge(k_psum, q + 1)
                    fn(ek[s][:], bank[7][:], ACT.Exp, bias=bqk[:, 1:2]).then_inc(qk_exp, 1)
                    act.wait_ge(kt_psum, q + 1)
                    fn(ktok[s][:], bank[7][:], ACT.Copy).then_inc(kt_ready, 1)

            def ffn(l):
                o = l * NBLK // 2

                def evict_x(s, n):
                    act.wait_ge(m["xgT_psum"][s], n + 1 + o)
                    act.wait_ge(m["gate_psum" if l else "up_psum"][s], n + o)
                    fn(xgT[s][:], bank[6][:, s * P:(s + 1) * P], ACT.Copy).then_inc(m["xgT_ready"][s], 1)

                def gelu(s, n):
                    if l == 0:
                        act.wait_ge(m["gate_psum"][s], n + 1 + o)
                        act.wait_ge(m["h_ready"][s], n + o)
                        fn(fa[s][:], bank[s][:], ACT.Gelu).then_inc(m["act_ready"][s], 1)
                    else:
                        act.wait_ge(m["pre_ready"][s], n + 1)
                        act.wait_ge(m["hT_psum"][s], n + o)
                        fn(fh[s][:], fa[s][:], ACT.Gelu).then_inc(m["h_ready"][s], 1)

                def store_y(s, n):
                    act.wait_ge(m["y_ready"][s], n + 1 + o)
                    act.dma_start(yg_d[bass.ds(n * 2 * P + s * P, P), :], yb[s][:]).then_inc(m["y_out"][s], 16)

                evict_x(0, 0)
                evict_x(1, 0)
                gelu(0, 0)
                evict_x(0, 1)
                gelu(1, 0)
                with act.Fori(0, NBLK // 2 - 2) as i:
                    evict_x(1, i + 1)
                    gelu(0, i + 1)
                    store_y(0, i)
                    evict_x(0, i + 2)
                    gelu(1, i + 1)
                    store_y(1, i)
                n = NBLK // 2 - 1
                evict_x(1, n)
                gelu(0, n)
                store_y(0, n - 1)
                gelu(1, n)
                store_y(1, n - 1)
                store_y(0, n)
                store_y(1, n)

            ffn(0)
            evict_xT(1)
            gap_exps(1)
            with act.Fori(0, B // 2) as i:
                for l in range(2):
                    for s in range(2):
                        act.wait_ge(gru_psum[l][s], i + 1)
                        act.wait_ge(gru_scan[1 - l][s], i + l)
                        fn(ga[s][:], bank[2 * s][:], ACT.Sigmoid, bias=bzh2[:, l:l + 1], scale=-1.0)
                        fn(gz[s][:], bank[2 * s][:], ACT.Sigmoid, bias=bzh[:, l:l + 1])
                        fn(gs[s][:], bank[2 * s + 1][:], ACT.Sigmoid, bias=bzh[:, 2 + l:3 + l]).then_inc(gru_act[l][s], 1)
            ffn(1)

        @block.vector
        def _(dve):
            v = nc.vector
            c = Chain(dve, dve_step)

            def three(a, n=E):
                return a.rearrange("p (t e) -> p t e", e=n)

            dve.wait_ge(small_in, NSMALL)
            c.add(v.tensor_scalar(bqke[:], bqk[:], FEAT_EPS, None, ALU.add))
            c.add(v.tensor_scalar(bzh2[:, 0:2], bzh[:, 0:2], -1.0, None, ALU.mult))
            c.add(v.tensor_scalar(bzh2[:, 2:4], bzh[:, 2:4], 0.5, None, ALU.add))
            c.add(v.reciprocal(rtemp[:], tempb[:]))
            c.link(v.tensor_tensor(out=simsq, in0=sim[:], in1=sim[:], op=ALU.mult))
            c.link(v.tensor_reduce(out=simn[:, 3:4], in_=simsq, axis=AX.X, op=ALU.add))
            v.tensor_scalar(simn[:, 0:1], simn[:, 3:4], NORM_EPS * NORM_EPS, None, ALU.max).then_inc(sim_sq, 1)
            dve.wait_ge(sim_pow, 1)
            v.tensor_scalar(sim[:], sim[:], simn[:, 1:2], None, ALU.mult).then_inc(simn_ready, 1)
            dve.wait_ge(simT_psum, 1)
            v.tensor_copy(simT[:], bank[7][:, 0:E]).then_inc(simT_ready, 1)

            def variances(stats, out, done):
                st6 = stats[:].rearrange("p (t k) -> p t k", k=6)
                a, b2, m2, mean, var = (out[:, k * NT:(k + 1) * NT] for k in (3, 4, 5, 0, 2))
                c.add(v.tensor_tensor(out=a, in0=st6[:, :, 1], in1=st6[:, :, 4], op=ALU.add))
                c.add(v.tensor_tensor(out=b2, in0=st6[:, :, 1], in1=st6[:, :, 4], op=ALU.subtract))
                c.link(v.tensor_tensor(out=m2, in0=st6[:, :, 2], in1=st6[:, :, 5], op=ALU.add))
                c.add(v.tensor_scalar(mean, a, 0.5, None, ALU.mult))
                c.link(v.tensor_tensor(out=b2, in0=b2, in1=b2, op=ALU.mult))
                c.link(v.scalar_tensor_tensor(out=m2, in0=b2, scalar=D / 4.0, in1=m2, op0=ALU.mult, op1=ALU.add))
                v.tensor_scalar(var, m2, 1.0 / D, LN_EPS, ALU.mult, ALU.add).then_inc(done, 1)

            def normalise(l):
                dve.wait_ge(rstd_ready[l], 1)
                with dve.Fori(0, B // 2) as i:
                    for s in range(2):
                        dve.wait_ge(xT_psum[l][s], i)
                        dve.wait_ge(xn_kept[l][s], i * 16)
                        for j in range(TPS):
                            t = i * 2 * TPS + (s * TPS + j)
                            v.tensor_scalar(xn_ring[s][:, j * D:(j + 1) * D], x[:, bass.ds(t * D, D)],
                                            ln[:, bass.ds(t, 1)], ln[:, bass.ds(t + NT, 1)],
                                            ALU.subtract, ALU.mult).then_inc(xn_ready[l][s], 1)

            def route(l):
                L = three(lg[:])
                eq_, cand, oh1, L2, oh2, tot, scan, dest = rt

                def per_tile(a):
                    return a[:].unsqueeze(2).to_broadcast([P, NT, E])

                revb = rev[:].unsqueeze(1).to_broadcast([P, NT, E])
                for scores, best, oh, r in ((lg, rs[0], oh1, rs[1]), (L2, rs[2], oh2, rs[3])):
                    c.link(v.tensor_reduce(out=best[:], in_=three(scores[:]), axis=AX.X, op=ALU.max))
                    c.link(v.tensor_tensor(out=three(eq_[:]), in0=three(scores[:]), in1=per_tile(best), op=ALU.is_equal))
                    c.link(v.tensor_tensor(out=three(cand[:]), in0=three(eq_[:]), in1=revb, op=ALU.mult))
                    c.link(v.tensor_reduce(out=r[:], in_=three(cand[:]), axis=AX.X, op=ALU.max))
                    c.link(v.tensor_tensor(out=three(oh[:]), in0=three(cand[:]), in1=per_tile(r), op=ALU.is_equal))
                    if oh is oh1:
                        c.link(v.scalar_tensor_tensor(out=L2[:], in0=oh1[:], scalar=-BIG, in1=lg[:], op0=ALU.mult,
                                                      op1=ALU.add))
                v.tensor_tensor(out=rs[4][:], in0=rs[2][:], in1=rs[0][:], op=ALU.subtract).then_inc(gap_ready[l], 1)
                v.tensor_tensor(out=m16[:].rearrange("p (e t) -> p t e", e=E), in0=three(oh1[:]), in1=three(oh2[:]),
                                op=ALU.add).then_inc(picks_ready[l], 1)
                dve.wait_ge(gap_exp[l], 1)
                c.link(v.tensor_scalar(rs[6][:], rs[5][:], 1.0, None, ALU.add))
                c.link(v.reciprocal(wgt[l][0][:], rs[6][:]))
                c.link(v.tensor_tensor(out=wgt[l][1][:], in0=rs[5][:], in1=wgt[l][0][:], op=ALU.mult))
                dve.wait_ge(ranks_psum[l], 1)
                c.link(v.tensor_copy(tot[:], bank[5][:, 256:512]))
                c.link(v.tensor_tensor_scan(out=scan[:], data0=ones[:, 0:256], data1=tot[:], initial=0.0,
                                            op0=ALU.mult, op1=ALU.add))
                c.link(v.memset(r9[:, 0:1], 0.0))
                c.link(v.tensor_copy(r9[:, 1:E + 1], scan[:].rearrange("p (e t) -> p e t", e=E)[:, :, NT - 1]))
                c.link(v.tensor_tensor(out=r8[0][:], in0=r9[:, 1:E + 1], in1=r9[:, 0:E], op=ALU.subtract))
                c.link(v.tensor_scalar(r8i[0][:], r8[0][:], float(P - 1), None, ALU.add))
                sh = P.bit_length() - 1
                c.link(v.tensor_scalar(r8i[1][:], r8i[0][:], sh, sh, ALU.logical_shift_right, ALU.logical_shift_left))
                c.link(v.tensor_copy(r8[1][:], r8i[1][:]))
                c.link(v.tensor_tensor_scan(out=r8[2][:], data0=ones[:, 0:E], data1=r8[1][:], initial=0.0,
                                            op0=ALU.mult, op1=ALU.add))
                c.link(v.tensor_tensor(out=r8[3][:], in0=r8[2][:], in1=r8[1][:], op=ALU.subtract))
                c.link(v.tensor_tensor(out=r8[4][:], in0=r8[3][:], in1=r9[:, 0:E], op=ALU.subtract))
                c.link(v.tensor_tensor(out=scan[:], in0=scan[:], in1=tot[:], op=ALU.subtract))
                c.link(v.tensor_tensor(out=scan[:], in0=scan[:], in1=bank[5][:, 0:256], op=ALU.add))
                c.link(v.tensor_tensor(out=dest[:].rearrange("p (e t) -> p e t", e=E),
                                       in0=scan[:].rearrange("p (e t) -> p e t", e=E),
                                       in1=r8[4][:].unsqueeze(2).to_broadcast([P, E, NT]), op=ALU.add))
                for k, oh in enumerate((oh1, oh2)):
                    c.link(v.tensor_tensor(out=three(cand[:]), in0=three(oh[:]),
                                           in1=dest[:].rearrange("p (e t) -> p t e", e=E), op=ALU.mult))
                    c.link(v.tensor_reduce(out=rs[7][:], in_=three(cand[:]), axis=AX.X, op=ALU.add))
                    c.link(v.tensor_copy(dst[l][k][:], rs[7][:]))
                c.link(v.tensor_tensor(out=three(cmpb[:]), in0=blk_start[:].unsqueeze(2).to_broadcast([1, NBLK, E]),
                                       in1=r8[2][0:1, :].unsqueeze(1).to_broadcast([1, NBLK, E]), op=ALU.is_ge))
                c.link(v.tensor_reduce(out=bexf[:], in_=three(cmpb[:]), axis=AX.X, op=ALU.add))
                v.tensor_scalar(bex[l][:], bexf[:], float(E - 1), None, ALU.min).then_inc(dest_ready[l], 1)

            for k in range(LOADS):
                dve.wait_ge(x_in[k], 16)
                with dve.Fori(k * TPL, (k + 1) * TPL) as t:
                    v.bn_stats(st[:, bass.ds(t * 6, 6)], x[:, bass.ds(t * D, D)]).then_inc(stats_done, 1)
            dve.wait_ge(stats_done, NT)
            variances(st, ln, var_ready[0])
            normalise(0)
            for s in range(2):
                dve.wait_ge(scored[0][s], B // 2)
            dve.wait_ge(consts_ready, 1)
            c.link(v.tensor_copy(lg[:], bank[4][:, 0:NT * E]))
            route(0)

            STEPS = 2 * 5
            dve.wait_ge(vpad_zeroed, 2)
            for s in range(2):
                dve.wait_ge(xn_kept[0][s], 16 * B // 2)
            with dve.Fori(0, B // 2) as i:
                c.enter(i, STEPS)
                for s in range(2):
                    q = i * 2 + s
                    dve.wait_ge(qk_exp, q * 2 + 1)
                    c.link(v.tensor_scalar(rq[s][:], bank[6][:], bqke[:, 0:1], FEAT_EPS, ALU.add, ALU.max))
                    v.scalar_tensor_tensor(out=qT[s][:], in0=eq[s][:], scalar=1.0, in1=rq[s][:], op0=ALU.min,
                                           op1=ALU.add).then_inc(q_ready, 1)
                    dve.wait_ge(qk_exp, q * 2 + 2)
                    c.link(v.tensor_scalar(rk[s][:], bank[7][:], bqke[:, 1:2], FEAT_EPS, ALU.add, ALU.max))
                    v.scalar_tensor_tensor(out=kT[s][:], in0=ek[s][:], scalar=1.0, in1=rk[s][:], op0=ALU.min,
                                           op1=ALU.add).then_inc(k_ready, 1)
                    dve.wait_ge(k_ready, q + 1)
                    dve.wait_ge(q_ready, q + 1)
                    dve.wait_ge(den_psum, q)
                    c.link(v.tensor_tensor_scan(out=kcum[:], data0=ones[:], data1=kT[s][:], initial=0.0,
                                                op0=ALU.mult, op1=ALU.add))
                    v.scalar_tensor_tensor(out=prod[:], in0=qT[s][:], scalar=HE ** -0.5, in1=kcum[:], op0=ALU.mult,
                                           op1=ALU.mult).then_inc(prod_ready, 1)
                    qv = qx[s].rearrange("p (t j n) -> p t j n", t=TPS, j=4)
                    for j in range(4):
                        ins = v.tensor_scalar(qv[:, :, j, :], qT[s][:].rearrange("p (t n) -> p t n", t=TPS),
                                              jmask[:, j:j + 1], None, ALU.mult)
                        if j == 3:
                            ins.then_inc(qx_ready, 1)
                    dve.wait_ge(v_psum, q + 1)
                    for j in range(TPS):
                        v.tensor_tensor(out=diag(vpad[s].rearrange("p (t n) -> p t n", t=TPS)[:, j, :]),
                                        in0=bank[6][:, j * P:(j + 1) * P].rearrange("p (g r c) -> p g r c", g=4, r=4),
                                        in1=bvb[:].rearrange("p (g r c) -> p g r c", g=4, r=4),
                                        op=ALU.add).then_inc(v_ready, 1)
                    dve.wait_ge(den_psum, q + 1)
                    v.tensor_scalar(dens[:], bank[6][:], FEAT_EPS, None, ALU.add).then_inc(den_read, 1)
                    dve.wait_ge(den_read, q + 1)
                    c.link(v.reciprocal(rden[:], dens[:]))
                    for j in range(TPS):
                        for g in range(4):
                            if g == 0 and j >= 2:
                                dve.wait_ge(num_psum, q * TPS + j - 1)
                            dve.wait_ge(score_psum, q * 16 + 4 * j + g + 1)
                            v.tensor_tensor(out=am[j % 2][:, g * S:(g + 1) * S].rearrange("p (r t) -> p r t", r=4),
                                            in0=bank[g][:].rearrange("p (r t) -> p r t", r=4),
                                            in1=tri[:].unsqueeze(1).to_broadcast([P, 4, P]),
                                            op=ALU.mult).then_inc(am_ready, 1)
                            if g == 0 and j < TPS - 1:
                                dve.wait_ge(kv_psum, q * (TPS - 1) + j + 1)
                                v.tensor_tensor(out=state[j % 2][:], in0=bank[5][:, 0:P], in1=headblk_q[:],
                                                op=ALU.mult).then_inc(state_ready, 1)
                    dve.wait_ge(num_psum, q * TPS + TPS)
                    v.tensor_tensor(out=attnT[s][:], in0=bank[4][:], in1=rden[:], op=ALU.mult).then_inc(attn_ready, 1)
                    dve.wait_ge(o_psum, q + 1)
                    v.tensor_tensor(out=attn_o[:, bass.ds(q * S, S)].rearrange("p (t d) -> p t d", d=D),
                                    in0=bank[7][:].rearrange("p (t d) -> p t d", d=D),
                                    in1=boutb[:].unsqueeze(1).to_broadcast([P, TPS, D]), op=ALU.add).then_inc(o_ready, 1)
                    dve.wait_ge(o_ready, q + 1)
                    for j in range(TPS):
                        t = q * TPS + j
                        ins = v.bn_stats(sto[:, bass.ds(t * 6, 6)], attn_o[:, bass.ds(t * D, D)])
                    c.add(ins)
                c.wait()
                assert c.n == STEPS, c.n
            c.leave(B // 2)
            variances(sto, lno, varo_ready)

            def ffn(l):
                o = l * NBLK // 2

                def hidden(s, n):
                    if l == 0:
                        dve.wait_ge(m["up_psum"][s], n + 1)
                        dve.wait_ge(m["act_ready"][s], n + 1)
                        dve.wait_ge(m["hT_psum"][s], n + o)
                        v.tensor_tensor(out=fh[s][:], in0=bank[2 + s][:], in1=fa[s][:], op=ALU.mult)\
                            .then_inc(m["h_ready"][s], 1)
                    else:
                        e = dve.value_load(bex[l][0:1, bass.ds(2 * n + s, 1)], min_val=0, max_val=E - 1)
                        dve.wait_ge(m["gate_psum"][s], n + 1 + o)
                        dve.wait_ge(m["h_ready"][s], n + o)
                        v.tensor_tensor(out=fa[s][:], in0=bank[s][:], in1=b1b[:, bass.ds(e * F, F)], op=ALU.add)\
                            .then_inc(m["pre_ready"][s], 1)

                def evict_h(s, n):
                    dve.wait_ge(m["hT_psum"][s], n + 1 + o)
                    dve.wait_ge(m["y_psum"][s], n + o)
                    v.tensor_copy(hT[s][:], bank[5][:]).then_inc(m["hT_ready"][s], 1)

                def evict_y(s, n):
                    if l:
                        e = dve.value_load(bex[l][0:1, bass.ds(2 * n + s, 1)], min_val=0, max_val=E - 1)
                    dve.wait_ge(m["y_psum"][s], n + 1 + o)
                    dve.wait_ge(m["y_out"][s], (n + o) * 16)
                    src = bank[7][:, s * P:(s + 1) * P]
                    if l == 0:
                        v.tensor_copy(yb[s][:], src).then_inc(m["y_ready"][s], 1)
                    else:
                        v.tensor_tensor(out=yb[s][:], in0=src, in1=b2b[:, bass.ds(e * D, D)], op=ALU.add)\
                            .then_inc(m["y_ready"][s], 1)

                hidden(0, 0)
                hidden(1, 0)
                evict_h(0, 0)
                with dve.Fori(0, NBLK // 2 - 2) as i:
                    hidden(0, i + 1)
                    evict_y(0, i)
                    evict_h(1, i)
                    hidden(1, i + 1)
                    evict_y(1, i)
                    evict_h(0, i + 1)
                n = NBLK // 2 - 1
                hidden(0, n)
                evict_y(0, n - 1)
                evict_h(1, n - 1)
                hidden(1, n)
                evict_y(1, n - 1)
                evict_h(0, n)
                evict_y(0, n)
                evict_h(1, n)
                evict_y(1, n)

            ffn(0)

            def combine(l, t):
                tok = bass.ds(t * D, D)
                c.link(v.scalar_tensor_tensor(out=x[:, tok], in0=gu[:, tok], scalar=wgt[l][0][:, bass.ds(t, 1)],
                                              in1=x[:, tok], op0=ALU.mult, op1=ALU.add))
                return v.scalar_tensor_tensor(out=x[:, tok], in0=gu[:, bass.ds(t * D + NT * D, D)],
                                              scalar=wgt[l][1][:, bass.ds(t, 1)],
                                              in1=x[:, tok], op0=ALU.mult, op1=ALU.add)

            dve.wait_ge(attn_added, 1)
            for k in range(LOADS):
                dve.wait_ge(gathered[0][k], 16 * 2 * TPL)
                with dve.Fori(0, TPL) as t0:
                    c.enter(t0, 2)
                    c.link(combine(0, t0 + k * TPL))
                    v.bn_stats(st[:, bass.ds(t0 * 6 + k * TPL * 6, 6)], x[:, bass.ds(t0 * D + k * TPL * D, D)])\
                        .then_inc(stats_done, 1)
                c.leave(TPL)
            dve.wait_ge(stats_done, 2 * NT)
            variances(st, ln, var_ready[1])
            normalise(1)
            for s in range(2):
                dve.wait_ge(scored[1][s], B // 2)
            c.link(v.tensor_scalar(rs[0][:], bank[6][:, 0:NT], NORM_EPS * NORM_EPS, None, ALU.max))
            v.tensor_copy(rs[1][:], rs[0][:]).then_inc(norm_ready, 1)
            dve.wait_ge(norm_pow, 1)
            c.link(v.tensor_scalar(rs[3][:], rs[2][:], rtemp[:], None, ALU.mult))
            c.link(v.tensor_tensor(out=three(lg[:]), in0=three(bank[4][:, 0:NT * E]),
                                   in1=rs[3][:].unsqueeze(2).to_broadcast([P, NT, E]), op=ALU.mult))
            route(1)

            with dve.Fori(0, B // 2) as i:
                c.enter(i, 2 * 2 * 2)
                for l in range(2):
                    for s in range(2):
                        h = (gh1, gh2)[l][s]
                        dve.wait_ge(gru_act[l][s], i + 1)
                        c.link(v.scalar_tensor_tensor(out=gs[s][:], in0=bank[2 * s + 1][:], scalar=bzh2[:, 2 + l:3 + l],
                                                      in1=gs[s][:], op0=ALU.add, op1=ALU.max))
                        c.link(v.tensor_tensor(out=gz[s][:], in0=gz[s][:], in1=gs[s][:], op=ALU.mult))
                        if l == 1:
                            dve.wait_ge(gruT_psum[s], i)
                        v.tensor_tensor_scan(out=h[:], data0=ga[s][:], data1=gz[s][:], initial=0.5,
                                             op0=ALU.mult, op1=ALU.add).then_inc(gru_scan[l][s], 1)
                for s in range(2):
                    tok = bass.ds(i * 2 * S + s * S, S)
                    dve.wait_ge(gruT_psum[s], i + 1)
                    v.tensor_tensor(out=x[:, tok], in0=x[:, tok], in1=bank[6 + s][:], op=ALU.add)\
                        .then_inc(gruT_added[s], 1)
            c.leave(B // 2)
            dve.wait_ge(w2_in, 48)
            ffn(1)
            for s in range(2):
                dve.wait_ge(gruT_added[s], B // 2)
            for k in range(LOADS):
                dve.wait_ge(gathered[1][k], 16 * 2 * TPL)
                with dve.Fori(0, TPL) as t0:
                    c.enter(t0, 2)
                    c.link(combine(1, t0 + k * TPL))
                c.leave(TPL)
                c.wait()
                v.memset(done_mark[:], 0.0).then_inc(out_ready[k], 1)


def kernel(**inputs):
    import numpy as _np
    import concourse.bacc as _bacc
    from concourse import mybir as _mybir
    from concourse.bass_utils import run_bass_kernel_spmd as _run

    a = {k: _np.asarray(v) for k, v in inputs.items()}
    wqkv = a["L0_attn_Wqkv"]
    laid = {
        "x": a["L0_attn_x"],
        "wqkv": wqkv.T,
        "bqk": a["L0_attn_bqkv"][:256].reshape(2, 128).T,
        "bv": a["L0_attn_bqkv"][256:],
        "wout": a["L0_attn_Wout"].T,
        "bout": a["L0_attn_bout"], "gamma": a["L0_attn_gamma"], "beta": a["L0_attn_beta"],
        "gatew": a["L0_ffn_gate_w"].T,
        "gu": a["L0_ffn_gate_up_w"].transpose(2, 0, 1).reshape(128, -1),
        "dw": a["L0_ffn_down_w"].reshape(8, 128, 4, 128).transpose(3, 0, 2, 1).reshape(128, -1),
        "wz": a["L1_attn_Wz"].transpose(2, 0, 1).reshape(128, -1), "bz": a["L1_attn_bz"].T,
        "wh": a["L1_attn_Wh"].transpose(2, 0, 1).reshape(128, -1), "bh": a["L1_attn_bh"].T,
        "wp": a["L1_ffn_Wp"].T, "sim": a["L1_ffn_sim_matrix"], "temp": a["L1_ffn_temperature"].reshape(1),
        "w1": a["L1_ffn_W1"].transpose(1, 0, 2).reshape(128, -1), "b1": a["L1_ffn_b1"].reshape(-1),
        "w2": a["L1_ffn_W2"].reshape(8, 4, 128, 128).transpose(2, 0, 1, 3).reshape(128, -1),
        "b2": a["L1_ffn_b2"].reshape(-1),
    }
    nc = _bacc.Bacc("TRN2", target_bir_lowering=False, num_devices=1)
    arrays, args = {}, []
    for name, v in laid.items():
        v = _np.ascontiguousarray(v)
        arrays[f"in_{name}"] = v
        args.append(nc.dram_tensor(f"in_{name}", v.shape, _mybir.dt.from_np(v.dtype), kind="ExternalInput").ap())
    f32 = _mybir.dt.float32
    args.append(nc.dram_tensor("sorted_tokens", (NBLK * P, D), f32, kind="Internal").ap())
    args.append(nc.dram_tensor("sorted_results", (NBLK * P, D), f32, kind="Internal").ap())
    args.append(nc.dram_tensor("out", (B, S, D), f32, kind="ExternalOutput").ap())
    build(nc, *args)
    return _run(nc, [arrays], core_ids=[0]).results[0]["out"]
```

```python
import concourse.bass as bass
from concourse import mybir
from concourse.alu_op_type import AluOpType as ALU
from contextlib import ExitStack

P = 128
B, S, D = 8, 512, 128
NT = B * S // P
TPS = S // P
H, HE = 16, 8
E, F = 8, 512
FC = F // P
NBLK = 2 * NT + E
ROW = D + 2
TAG, WGT = D, D + 1
FEAT_EPS = 1e-4
LN_EPS = 1e-5
NORM_EPS = 1e-12
LOADS = 4
TPL = NT // LOADS
NXG, NYB = 6, 4
BIG = 3.0e38


class Chain:

    def __init__(self, engine, sem):
        self.engine, self.sem, self.n = engine, sem, 0

    def add(self, ins):
        ins.then_inc(self.sem, 1)
        self.n += 1

    def wait(self):
        self.engine.wait_ge(self.sem, self.n)

    def link(self, ins):
        self.add(ins)
        self.wait()


def after(engine, sem, n):
    if n > 0:
        engine.wait_ge(sem, n)


def build(nc, x_d, wqkv_d, bqkv_d, wout_d, bout_d, gamma_d, beta_d, gatew_d, gu_d, dw_d,
          wz_d, bz_d, wh_d, bh_d, wp_d, sim_d, temp_d, w1_d, b1_d, w2_d, b2_d, list0_d, list1_d, res_d, out_d):
    fp32, bf16 = mybir.dt.float32, mybir.dt.bfloat16
    i32, u32 = mybir.dt.int32, mybir.dt.uint32
    ACT = mybir.ActivationFunctionType
    AX = mybir.AxisListType

    ctx = ExitStack()
    with ctx:
        def sb(name, shape, dt=fp32):
            return ctx.enter_context(nc.sbuf_tensor(name, shape, dt))

        def sem(name):
            return ctx.enter_context(nc.semaphore(name))

        def sems(name, n=2):
            return [sem(f"{name}{k}") for k in range(n)]

        x = sb("x", [P, NT * D])
        xn = sb("xn", [P, NT * ROW])
        xnT = sb("xnT", [P, NT * P])
        attn_o = xnT
        gu = sb("gu", [P, E * 2 * F])
        dw = sb("dw", [P, E * FC * D])
        y = [gu[:, k * NT * D:(k + 1) * NT * D] for k in range(2)]
        big = sb("big", [P, 3 * NT * D])
        w1 = big[:, 0:E * F]
        w2 = big[:, E * F:2 * E * F]
        b1b = big[:, 2 * E * F:3 * E * F]
        b2b = sb("b2b", [P, E * D])
        scr = sb("scr", [P, 6144])
        qTb = sb("qTb", [P, 2 * S])
        tmp = sb("tmp", [P, 2048])
        ident = sb("ident", [P, P])
        ones = sb("ones", [P, NT * E])
        tri = sb("tri", [P, P])
        smask = sb("smask", [P, P + H])
        nostate = sb("nostate", [P, P + H])
        upper16 = sb("upper16", [P, P], bf16)
        ones16 = sb("ones16", [P, P], bf16)
        rev = sb("rev", [P, E])
        blk_start = sb("blk_start", [1, NBLK])
        wqkv = sb("wqkv", [P, 3 * D])
        wout = sb("wout", [P, D])
        gatew = sb("gatew", [P, E])
        wz = sb("wz", [P, 2 * D])
        wh = sb("wh", [P, 2 * D])
        wp = sb("wp", [P, D])
        bzh = sb("bzh", [P, 4])
        bzh2 = sb("bzh2", [P, 4])
        bqkvb = sb("bqkvb", [P, 3 * D])
        boutr = sb("boutr", [1, D])
        gammab = sb("gammab", [P, D])
        betab = sb("betab", [P, D])
        tempb = sb("tempb", [P, 1])
        rtemp = sb("rtemp", [P, 1])
        sim = sb("sim", [E, D])
        simn = sb("simn", [E, 4])
        simT = sb("simT", [P, E])
        state = sb("state", [P, 2 * (P + H)])
        st = sb("st", [P, NT * 6])
        sto = sb("sto", [P, NBLK * E])
        ln = sb("ln", [P, 8 * NT])
        lg = sb("lg", [P, NT * E])
        rs = [sb(f"rs{k}", [P, NT]) for k in range(8)]
        r9 = sb("r9", [P, E + 1])
        r8 = [sb(f"r8_{k}", [P, E]) for k in range(5)]
        r8i = [sb(f"r8i_{k}", [P, E], i32) for k in range(2)]
        m16 = sb("m16", [P, NT * E], bf16)
        wgt = [sb(f"wgt{k}", [P, NT]) for k in range(2)]
        dst = [[sb(f"dst{l}_{k}", [P, NT], u32) for k in range(2)] for l in range(2)]
        bexf = sb("bexf", [1, NBLK])
        bex = [sb(f"bex{l}", [1, NBLK], i32) for l in range(2)]

        def part(a, at, size, n):
            return [a[:, at + k * size:at + (k + 1) * size] for k in range(n)]

        rt = part(tmp, 0, NT * E, 8)
        ex = part(scr, 0, S, 2)
        kvx = part(scr, 0, 1024, 2)
        pr = part(scr, 2048, 1024, 2)
        red = scr[:, 4096:4608]
        att = scr[:, 4608:5120]
        kq = scr[:, 5120:5632]
        aT = scr[:, 5632:6144]
        dred, sden, rden = part(lg, 0, TPS * H, 3)
        qT = part(qTb, 0, S, 2)
        stt = part(state, 0, P + H, 2)
        fa = part(scr, 0, F, 2)
        fh = part(scr, 1024, F, 2)
        hT = part(scr, 2048, F, 2)
        xg = part(scr, 3072, ROW, NXG)
        xgT = part(scr, 3072 + NXG * ROW, P, 2)
        yb = part(scr, 3072 + NXG * ROW + 2 * P, D, NYB)
        projT, sq = part(scr, 0, S, 2), part(scr, 1024, S, 2)
        ga, gz, gs, gh1, gh2 = (part(scr, 1024 * k, S, 2) for k in range(5))

        def col(a, k):
            return a.rearrange("p (t r) -> p t r", r=ROW)[:, :, k]

        NG = gu.shape[1] // ROW
        FILL = [(gu[:, 0:NG * ROW], 0, NG), (dw[:, 0:(NBLK - NG) * ROW], NG, NBLK - NG)]

        ps = ctx.enter_context(nc.psum_tensor("ps", [P, 8 * 512], fp32))
        bank = part(ps, 0, 512, 8)

        x_in = sems("x_in", LOADS)
        small_in, gu_in, dw_in, w2_in = sem("small_in"), sem("gu_in"), sem("dw_in"), sem("w2_in")
        list_filled = sems("list_filled")
        pool_step, dve_step = sem("pool_step"), sem("dve_step")
        consts_ready, fill_ready = sem("consts_ready"), sem("fill_ready")
        var_ready, sqrt_ready = sem("var_ready"), sem("sqrt_ready")
        rstd_ready = sem("rstd_ready")
        xn_dve, xn_act = sem("xn_dve"), sem("xn_act")
        xT_psum, xT_ready, scored = sem("xT_psum"), sem("xT_ready"), sem("scored")
        proj_psum, proj_ready = sem("proj_psum"), sem("proj_ready")
        gap_ready, gap_exp, picks_ready = sem("gap_ready"), sem("gap_exp"), sem("picks_ready")
        weights_ready = sem("weights_ready")
        ranks_psum, dest_ready = sem("ranks_psum"), sem("dest_ready")
        norms_ready, sim_sq, sim_root = sem("norms_ready"), sem("sim_sq"), sem("sim_root")
        listed = sems("listed", 4)
        simn_ready, simT_psum, simT_ready = sem("simn_ready"), sem("simT_psum"), sem("simT_ready")
        qkv_psum, qkv_biased, feat_exp, feat_ready = sem("qkv_psum"), sem("qkv_biased"), sem("feat_exp"), sem("feat_ready")
        kvx_ready, tri_psum, prod_ready = sem("kvx_ready"), sem("tri_psum"), sem("prod_ready")
        kq_ready, state_psum, state_ready = sem("kq_ready"), sem("state_psum"), sem("state_ready")
        inter_psum, sums_ready, att_ready = sem("inter_psum"), sem("sums_ready"), sem("att_ready")
        qT_psum, qT_ready, aT_psum, aT_ready = sem("qT_psum"), sem("qT_ready"), sem("aT_psum"), sem("aT_ready")
        o_psum, o_ready = sem("o_psum"), sem("o_ready")
        o_normed, attn_added = sem("o_normed"), sem("attn_added")
        xg_in = sems("xg_in", NXG)
        xgT_psum, xgT_ready = sem("xgT_psum"), sem("xgT_ready")
        gate_psum, up_psum, act_ready, pre_ready = sem("gate_psum"), sem("up_psum"), sem("act_ready"), sem("pre_ready")
        h_ready, hT_psum, hT_ready = sem("h_ready"), sem("hT_psum"), sem("hT_ready")
        y_psum, y_ready = sem("y_psum"), sem("y_ready")
        y_out = sems("y_out", NYB)
        y_in = [sems(f"y_in{l}_", LOADS) for l in range(2)]
        stats_ready, x_added = sem("stats_ready"), sem("x_added")
        gru_psum, gru_act, gru_scan = sem("gru_psum"), sem("gru_act"), sem("gru_scan")
        gruT_psum, gruT_added = sem("gruT_psum"), sem("gruT_added")
        out_ready, stored = sem("out_ready"), sem("stored")

        block = ctx.enter_context(nc.Block())

        SMALL = [(wqkv, wqkv_d), (wout, wout_d), (gatew, gatew_d), (wz, wz_d), (wh, wh_d), (wp, wp_d),
                 (boutr, bout_d), (bzh[:, 0:2], bz_d), (bzh[:, 2:4], bh_d), (sim, sim_d)]
        BCAST = [(bqkvb, bqkv_d), (gammab, gamma_d), (betab, beta_d), (tempb, temp_d), (b2b, b2_d)]
        NSMALL = 16 * (len(SMALL) + len(BCAST))
        x_rows = x_d.rearrange("b (c p) d -> p (b c) d", p=P)
        out_rows = out_d.rearrange("b (c p) d -> p (b c) d", p=P)
        res_rows = res_d[0:2 * NT * P, :].rearrange("(t p) d -> p t d", p=P)
        lists = [list0_d, list1_d]

        def group(a, k, n=TPL):
            return a[:, k * n * D:(k + 1) * n * D].rearrange("p (t d) -> p t d", d=D)

        order = [(0, 0), (0, 1)]
        for g in range(B):
            order.append((1, g))
            if g + 2 < B:
                order.append((0, g + 2))

        @block.sync
        def _(sp):
            for k in range(LOADS):
                sp.dma_start(group(x, k), x_rows[:, k * TPL:(k + 1) * TPL, :]).then_inc(x_in[k], 16)

            sp.wait_ge(fill_ready, len(FILL))
            for l in range(2):
                for src, c0, n in FILL:
                    sp.dma_start(lists[l].rearrange("(p c) r -> p (c r)", p=P)[:, c0 * ROW:(c0 + n) * ROW], src)\
                        .then_inc(list_filled[l], 16)
            for l in range(2):
                sp.wait_ge(list_filled[l], 16 * len(FILL))
            sp.dma_start(gu[:], gu_d).then_inc(gu_in, 16)
            sp.dma_start(dw[:], dw_d).then_inc(dw_in, 16)

            def load_blocks(l):
                for k in range(2):
                    sp.wait_ge(listed[2 * l + k], 16 * NT)
                for b in range(NBLK):
                    n = l * NBLK + b
                    if b >= NXG:
                        sp.wait_ge(y_out[(n - NXG) % NYB], 16 * ((n - NXG) // NYB + 1))
                    sp.dma_start(xg[n % NXG], lists[l][b * P:(b + 1) * P, :]).then_inc(xg_in[n % NXG], 16)
                    if l == 0 and 8 <= b < 8 + E:
                        e = b - 8
                        for to, src in ((w1, w1_d), (w2, w2_d)):
                            sp.dma_start(to[:, e * F:(e + 1) * F], src[:, e * F:(e + 1) * F]).then_inc(w2_in, 16)
                        sp.dma_start(b1b[:, e * F:(e + 1) * F], b1_d[e * F:(e + 1) * F].partition_broadcast(P))\
                            .then_inc(w2_in, 16)

            def load_results(l):
                n = (l + 1) * NBLK
                for s in range(NYB):
                    sp.wait_ge(y_out[s], 16 * n // NYB)
                if l == 0:
                    sp.wait_ge(y_psum, n)
                else:
                    sp.wait_ge(x_added, LOADS)
                for k in range(LOADS):
                    for p in range(2):
                        sp.dma_start(group(y[p], k), res_rows[:, p * NT + k * TPL:p * NT + (k + 1) * TPL, :])\
                            .then_inc(y_in[l][k], 16)

            sp.wait_ge(aT_ready, B)
            load_blocks(0)
            load_results(0)
            sp.wait_ge(gruT_psum, B)
            load_blocks(1)
            load_results(1)
            for k in range(LOADS):
                sp.wait_ge(out_ready, k + 1)
                sp.dma_start(out_rows[:, k * TPL:(k + 1) * TPL, :], group(x, k)).then_inc(stored, 16)
            sp.wait_ge(stored, 16 * LOADS)

        @block.gpsimd
        def _(pool):
            c = Chain(pool, pool_step)
            for src, c0, n in FILL:
                c.link(pool.memset(src, 0.0))
                pool.iota(col(src.bitcast(i32), TAG), [[1, n]], base=2 * NT * P + c0, channel_multiplier=NBLK)\
                    .then_inc(fill_ready, 1)
            for to, v in ((ident, 0.0), (ones, 1.0), (tri, 1.0), (smask, 1.0), (upper16, 1.0), (ones16, 1.0),
                          (nostate, 0.0)):
                c.add(pool.memset(to[:], v))
            c.wait()

            def select(t, pattern, base, mult, op, value):
                c.add(pool.affine_select(out=t, in_=t, compare_op=op, fill=value, base=base, pattern=pattern,
                                         channel_multiplier=mult))

            select(ident[:], [[-1, P]], 0, 1, ALU.not_equal, 1.0)
            select(tri[:], [[1, P]], 0, -1, ALU.is_ge, 0.0)
            select(upper16[:], [[1, P]], -1, -1, ALU.is_ge, 0.0)
            blocks = smask[:, 0:P].rearrange("p (h c) -> p h c", c=HE)
            heads = smask[:, P:P + H].unsqueeze(2)
            for v, w in ((blocks, HE), (heads, 1)):
                select(v, [[-HE, H], [0, w]], 0, 1, ALU.is_ge, 0.0)
            c.wait()
            for v, w in ((blocks, HE), (heads, 1)):
                select(v, [[HE, H], [0, w]], HE - 1, -1, ALU.is_ge, 0.0)
            c.add(pool.iota(blk_start[:], [[P, NBLK]], base=0, channel_multiplier=0,
                            allow_small_or_imprecise_dtypes=True))
            c.add(pool.iota(rev[:], [[-1, E]], base=E, channel_multiplier=0, allow_small_or_imprecise_dtypes=True))
            c.wait()
            pool.memset(r9[:, 0:1], 0.0).then_inc(consts_ready, 1)

            def tag(l, k):
                if 2 * l + k:
                    pool.wait_ge(listed[2 * l + k - 1], 16 * NT)
                c.link(pool.iota(col(xn[:].bitcast(i32), TAG), [[P, NT]], base=k * NT * P, channel_multiplier=1))
                if k == 0:
                    pool.wait_ge(weights_ready, l + 1)
                c.link(pool.tensor_copy(col(xn[:], WGT), wgt[k][:]))

            def scatter(l):
                tag(l, 0)
                pool.wait_ge(dest_ready, l + 1)
                pool.wait_ge(xn_dve, (l + 1) * NT // 2)
                pool.wait_ge(xn_act, (l + 1) * NT // 2)
                pool.wait_ge(list_filled[l], 16 * len(FILL))
                for k in range(2):
                    if k:
                        tag(l, 1)
                    for t in range(NT):
                        pool.indirect_dma_start(lists[l], bass.IndirectOffsetOnAxis(ap=dst[l][k][:, t:t + 1], axis=0),
                                                xn[:, t * ROW:(t + 1) * ROW], None).then_inc(listed[2 * l + k], 16)

            def put_result(n):
                pool.wait_ge(y_ready, n + 1)
                pool.indirect_dma_start(res_d, bass.IndirectOffsetOnAxis(ap=xg[n % NXG][:, TAG:TAG + 1].bitcast(u32), axis=0),
                                        yb[n % NYB], None).then_inc(y_out[n % NYB], 16)

            scatter(0)
            beta4 = betab[:].unsqueeze(1).to_broadcast([P, TPS, D])
            gamma4 = gammab[:].unsqueeze(1).to_broadcast([P, TPS, D])
            for g in range(B):
                c.add(pool.tensor_tensor(out=group(x, g, TPS), in0=group(x, g, TPS), in1=beta4, op=ALU.add))
            c.wait()
            for n in range(NBLK):
                put_result(n)
                if n % 8 == 7 and n // 8 < B:
                    g = n // 8
                    pool.wait_ge(o_normed, (g + 1) * TPS)
                    o = group(attn_o, g, TPS)
                    c.link(pool.tensor_tensor(out=o, in0=o, in1=gamma4, op=ALU.mult))
                    pool.tensor_tensor(out=group(x, g, TPS), in0=group(x, g, TPS), in1=o, op=ALU.add)\
                        .then_inc(attn_added, 1)
            scatter(1)
            for n in range(NBLK, 2 * NBLK):
                put_result(n)

        @block.tensor
        def _(pe):
            mm, xpose = nc.tensor.matmul, nc.tensor.transpose
            pe.wait_ge(consts_ready, 1)
            pe.wait_ge(small_in, NSMALL)

            def cols(j, n=P):
                return slice(j * n, (j + 1) * n)

            def to_channels(l):
                for g in range(B + 1):
                    if g < B:
                        n = l * B + g
                        pe.wait_ge(xn_dve, (n + 1) * TPS // 2)
                        pe.wait_ge(xn_act, (n + 1) * TPS // 2)
                        after(pe, xT_ready, n - 1)
                        for j in range(TPS):
                            t = g * TPS + j
                            ins = xpose(bank[g % 2][:, cols(j)], xn[:, t * ROW:t * ROW + D], ident[:])
                        ins.then_inc(xT_psum, 1)
                    if g > 0:
                        yield g - 1

            for g in to_channels(0):
                pe.wait_ge(xT_ready, g + 1)
                for j in range(TPS):
                    t = g * TPS + j
                    ins = mm(bank[4][:, cols(t, E)], xnT[:, cols(t)], gatew[:], start=True, stop=True)
                ins.then_inc(scored, 1)

            def ranks(l):
                pe.wait_ge(picks_ready, l + 1)
                mm(bank[5][:, 0:256], upper16[:], m16[:], start=True, stop=True)
                mm(bank[5][:, 256:512], ones16[:], m16[:], start=True, stop=True).then_inc(ranks_psum, 1)

            PAIRS = (0, 2, 6)
            for u in range(NT // 2):
                if u == 2:
                    ranks(0)
                after(pe, qkv_biased, u - 2)
                for k in range(2):
                    t = 2 * u + k
                    ins = mm(bank[PAIRS[u % 3] + k][:, 0:3 * D], xnT[:, cols(t)], wqkv[:], start=True, stop=True)
                ins.then_inc(qkv_psum, 1)

            def qkv(t, k):
                return big[:, (3 * t + k) * D:(3 * t + k + 1) * D]

            def running(t):
                j, pair = t % TPS, 2 * (t % 2)
                pe.wait_ge(kvx_ready, t + 1)
                after(pe, prod_ready, t - 1)
                mm(bank[pair], tri[:], kvx[t % 2][:, 0:512], start=True, stop=True)
                mm(bank[pair + 1], tri[:], kvx[t % 2][:, 512:1024], start=True, stop=True)
                if j == 0:
                    after(pe, kq_ready, t // TPS)
                mm(bank[6][:, cols(j)], tri[:], qkv(t, 1), start=True, stop=True).then_inc(tri_psum, 1)

            def across(t):
                g, j = t // TPS, t % TPS
                before = stt[(t - 1) % 2] if j else nostate[:]
                after(pe, state_ready, g * (TPS - 1) + j)
                lhs = qT[g % 2][:, cols(j)]
                mm(bank[7][:, cols(j)], lhs, before[:, 0:P], start=True, stop=True)
                ins = mm(bank[5][:, 256 + j * H:256 + (j + 1) * H], lhs, before[:, P:P + H], start=True, stop=True,
                         skip_group_check=True)
                if j == TPS - 1:
                    ins.then_inc(inter_psum, 1)
                else:
                    mm(bank[5][:, 0:P], qkv(t, 1), qkv(t, 2), start=True, stop=True, skip_group_check=True)
                    mm(bank[5][:, P:P + H], qkv(t, 1), ones[:, 0:H], start=True, stop=True,
                       skip_group_check=True).then_inc(state_psum, 1)

            def project(g):
                pe.wait_ge(att_ready, g + 1)
                pe.wait_ge(qT_ready, g + 1)
                for j in range(TPS):
                    ins = xpose(bank[4][:, cols(j)], att[:, cols(j)], ident[:])
                ins.then_inc(aT_psum, 1)
                pe.wait_ge(aT_ready, g + 1)
                for j in range(TPS):
                    mm(bank[4][:, cols(j)], ones[0:1, 0:P], boutr[:], start=True, stop=False)
                    ins = mm(bank[4][:, cols(j)], aT[:, cols(j)], wout[:], start=False, stop=True)
                ins.then_inc(o_psum, 1)

            for g in range(B):
                t = g * TPS
                running(t)
                running(t + 1)
                if g:
                    project(g - 1)
                    pe.wait_ge(o_ready, g)
                if g == 0:
                    pe.wait_ge(dest_ready, 1)
                for j in range(TPS):
                    ins = xpose(bank[4][:, cols(j)], qkv(t + j, 0), ident[:])
                ins.then_inc(qT_psum, 1)
                pe.wait_ge(qT_ready, g + 1)
                after(pe, sums_ready, g)
                across(t)
                running(t + 2)
                across(t + 1)
                running(t + 3)
                across(t + 2)
                across(t + 3)
            project(B - 1)

            def ffn(l):
                wa, wb, wid = (gu, dw[:], 2 * F) if l == 0 else (w1, w2, F)
                first = l * NBLK

                def load_xpose(n):
                    pe.wait_ge(xg_in[n % NXG], 16 * (n // NXG + 1))
                    after(pe, xgT_ready, n)
                    xpose(bank[6][:, cols(n % 2)], xg[n % NXG][:, 0:D], ident[:]).then_inc(xgT_psum, 1)

                def expert(n):
                    return pe.value_load(bex[l][0:1, n - first:n - first + 1], min_val=0, max_val=E - 1)

                def up(n, e):
                    pe.wait_ge(xgT_ready, n + 1)
                    after(pe, pre_ready if l else act_ready, n - first - 1)
                    mm(bank[n % 2], xgT[n % 2], wa[:, bass.ds(e * wid, F)], start=True, stop=True).then_inc(gate_psum, 1)
                    if l == 0:
                        after(pe, h_ready, n - 1)
                        mm(bank[2 + n % 2], xgT[n % 2], wa[:, bass.ds(e * wid + F, F)], start=True, stop=True)\
                            .then_inc(up_psum, 1)

                def down(n, e):
                    pe.wait_ge(hT_ready, n + 1)
                    after(pe, y_ready, n)
                    for fc in range(FC):
                        ins = mm(bank[7][:, cols(n % 2)], hT[n % 2][:, cols(fc)],
                                 wb[:, bass.ds(e * FC * D + fc * D, D)], start=(fc == 0), stop=(fc == FC - 1))
                    ins.then_inc(y_psum, 1)

                def xpose_h(n):
                    pe.wait_ge(h_ready, n + 1)
                    after(pe, hT_ready, n)
                    for fc in range(FC):
                        ins = xpose(bank[5][:, cols(fc)], fh[n % 2][:, cols(fc)], ident[:])
                    ins.then_inc(hT_psum, 1)

                load_xpose(first)
                e = {}
                for b in range(NBLK + 2):
                    n = first + b
                    if b + 1 < NBLK:
                        load_xpose(n + 1)
                    if b < NBLK:
                        e[b] = expert(n)
                        up(n, e[b])
                    if b >= 2:
                        down(n - 2, e.pop(b - 2))
                    if 1 <= b <= NBLK:
                        xpose_h(n - 1)

            pe.wait_ge(simn_ready, 1)
            xpose(bank[7][:, 0:E], sim[:], ident[0:E, 0:E]).then_inc(simT_psum, 1)
            pe.wait_ge(simT_ready, 1)
            pe.wait_ge(gu_in, 16)
            pe.wait_ge(dw_in, 16)
            pe.wait_ge(o_ready, B)
            ffn(0)


            def scores(g):
                pe.wait_ge(proj_ready, g + 1)
                for j in range(TPS):
                    t = g * TPS + j
                    mm(bank[4][:, cols(t, E)], projT[g % 2][:, cols(j)], simT[:], start=True, stop=True)
                    ins = mm(bank[6][:, t:t + 1], sq[g % 2][:, cols(j)], ones[:, 0:1], start=True, stop=True)
                ins.then_inc(scored, 1)

            for g in to_channels(1):
                pe.wait_ge(xT_ready, B + g + 1)
                after(pe, proj_ready, g - 1)
                mm(bank[2 + g % 2], wp[:], xnT[:, cols(g, S)], start=True, stop=True).then_inc(proj_psum, 1)
                if g:
                    scores(g - 1)
            scores(B - 1)

            def gru(l, g):
                n = 2 * g + l if g else l
                s = l
                after(pe, gru_scan, order.index((l, g - 1)) + 1 if g else 0)
                if l:
                    pe.wait_ge(gru_scan, order.index((0, g)) + 1)
                rhs = xnT[:, cols(g, S)] if l == 0 else gh1[g % 2]
                mm(bank[2 * s], wz[:, cols(l)], rhs, start=True, stop=True)
                mm(bank[2 * s + 1], wh[:, cols(l)], rhs, start=True, stop=True).then_inc(gru_psum, 1)

            def gru_out(g):
                pe.wait_ge(gru_scan, order.index((1, g)) + 1)
                after(pe, gruT_added, g)
                for j in range(TPS):
                    ins = xpose(bank[7][:, cols(j)], gh2[g % 2][:, cols(j)], ident[:])
                ins.then_inc(gruT_psum, 1)

            gru(0, 0)
            ranks(1)
            gru(0, 1)
            for g in range(B):
                gru(1, g)
                if g + 2 < B:
                    gru(0, g + 2)
                gru_out(g)
            pe.wait_ge(w2_in, 16 * 3 * E)
            pe.wait_ge(gruT_added, B)
            pe.wait_ge(dest_ready, 2)
            ffn(1)

        @block.scalar
        def _(act):
            fn = nc.scalar.activation
            for to, src in SMALL:
                act.dma_start(to[:], src).then_inc(small_in, 16)
            for to, src in BCAST:
                act.dma_start(to[:], src.partition_broadcast(P)).then_inc(small_in, 16)

            def normalise(l, t):
                fn(xn[:, t * ROW:t * ROW + D], x[:, t * D:(t + 1) * D], ACT.Identity, bias=ln[:, 2 * NT + t:2 * NT + t + 1],
                   scale=ln[:, NT + t:NT + t + 1]).then_inc(xn_act, 1)

            def tokens(l):
                for k in range(LOADS):
                    act.wait_ge(var_ready, (LOADS + 1) * l + k + 1)
                    c8 = slice(3 * NT + k * TPL, 3 * NT + (k + 1) * TPL)
                    d8 = slice(4 * NT + k * TPL, 4 * NT + (k + 1) * TPL)
                    fn(ln[:, d8], ln[:, c8], ACT.Sqrt).then_inc(sqrt_ready, 1)
                if l:
                    for p in range(2):
                        act.wait_ge(listed[p], 16 * NT)

                def normalise_group(k):
                    act.wait_ge(rstd_ready, (LOADS + 1) * l + k + 1)
                    for t in range(k * TPL + 1, (k + 1) * TPL, 2):
                        normalise(l, t)

                normalise_group(0)
                for k in range(LOADS):
                    if k + 1 < LOADS:
                        normalise_group(k + 1)
                    for g in range(k * TPL // TPS, (k + 1) * TPL // TPS):
                        act.wait_ge(xT_psum, l * B + g + 1)
                        fn(xnT[:, g * S:(g + 1) * S], bank[g % 2], ACT.Copy).then_inc(xT_ready, 1)
                        if l == 1:
                            act.wait_ge(proj_psum, g + 1)
                            after(act, scored, B + g - 1)
                            fn(projT[g % 2], bank[2 + g % 2], ACT.Copy)
                            fn(sq[g % 2], bank[2 + g % 2], ACT.Square).then_inc(proj_ready, 1)

            def gap_exps(l):
                act.wait_ge(gap_ready, l + 1)
                fn(rs[5][:], rs[4][:], ACT.Exp).then_inc(gap_exp, 1)

            act.wait_ge(var_ready, 1)
            tokens(0)
            gap_exps(0)
            for u in range(NT // 2):
                act.wait_ge(qkv_biased, u + 1)
                after(act, feat_ready, u - 1)
                qk = big[:, 2 * u * 3 * D:(2 * u + 2) * 3 * D].rearrange("p (t c) -> p t c", t=2)[:, :, 0:2 * D]
                fn(ex[u % 2].rearrange("p (t c) -> p t c", t=2), qk, ACT.Exp).then_inc(feat_exp, 1)

            def project(g):
                act.wait_ge(aT_psum, g + 1)
                fn(aT, bank[4], ACT.Copy).then_inc(aT_ready, 1)
                act.wait_ge(o_psum, g + 1)
                fn(attn_o[:, g * S:(g + 1) * S], bank[4], ACT.Copy).then_inc(o_ready, 1)

            for g in range(B):
                if g:
                    project(g - 1)
                act.wait_ge(qT_psum, g + 1)
                fn(qT[g % 2], bank[4], ACT.Copy).then_inc(qT_ready, 1)
            act.wait_ge(sim_sq, 1)
            fn(simn[:, 1:2], simn[:, 0:1], ACT.Sqrt).then_inc(sim_root, 1)
            project(B - 1)
            act.wait_ge(var_ready, LOADS + 1)
            fn(ln[:, 4 * NT:5 * NT], ln[:, 3 * NT:4 * NT], ACT.Sqrt).then_inc(sqrt_ready, 1)

            def ffn(l):
                first = l * NBLK

                def evict_x(n):
                    act.wait_ge(xgT_psum, n + 1)
                    if l:
                        after(act, gate_psum, n - 1)
                    else:
                        after(act, up_psum, n - 1)
                    fn(xgT[n % 2], bank[6][:, (n % 2) * P:(n % 2 + 1) * P], ACT.Copy).then_inc(xgT_ready, 1)

                evict_x(first)
                for b in range(NBLK):
                    n = first + b
                    if b + 1 < NBLK:
                        evict_x(n + 1)
                    if l == 0:
                        act.wait_ge(gate_psum, n + 1)
                        after(act, h_ready, n - 1)
                        fn(fa[n % 2], bank[n % 2], ACT.Gelu).then_inc(act_ready, 1)
                        if b % 2 and b // 2 < NT:
                            t0 = b // 2
                            if t0 == 0:
                                act.wait_ge(rstd_ready, LOADS + 1)
                            fn(attn_o[:, t0 * D:(t0 + 1) * D], attn_o[:, t0 * D:(t0 + 1) * D], ACT.Identity,
                               bias=ln[:, 2 * NT + t0:2 * NT + t0 + 1], scale=ln[:, NT + t0:NT + t0 + 1]).then_inc(o_normed, 1)
                    else:
                        act.wait_ge(pre_ready, b + 1)
                        after(act, hT_psum, n - 1)
                        fn(fh[n % 2], fa[n % 2], ACT.Gelu).then_inc(h_ready, 1)

            ffn(0)
            tokens(1)
            act.wait_ge(norms_ready, 1)
            fn(rs[2][:], rs[0][:], ACT.Sqrt).then_inc(sqrt_ready, 1)
            gap_exps(1)
            for n, (l, g) in enumerate(order):
                act.wait_ge(gru_psum, n + 1)
                s = g % 2
                last = max([k for k in range(n) if order[k][1] % 2 == s], default=-1)
                after(act, gru_scan, last + 1)
                fn(ga[s], bank[2 * l], ACT.Sigmoid, bias=bzh2[:, l:l + 1], scale=-1.0)
                fn(gz[s], bank[2 * l], ACT.Sigmoid, bias=bzh[:, l:l + 1])
                fn(gs[s], bank[2 * l + 1], ACT.Sigmoid, bias=bzh[:, 2 + l:3 + l]).then_inc(gru_act, 1)
            ffn(1)

        @block.vector
        def _(dve):
            v = nc.vector
            c = Chain(dve, dve_step)

            def three(a, n=E):
                return a.rearrange("p (t e) -> p t e", e=n)

            def variances(stats, k0, k1):
                st6 = stats[:, k0 * 6:k1 * 6].rearrange("p (t k) -> p t k", k=6)
                mean, var, a, b2, m2 = (ln[:, k * NT + k0:k * NT + k1] for k in (0, 3, 5, 6, 7))
                c.add(v.tensor_tensor(out=a, in0=st6[:, :, 1], in1=st6[:, :, 4], op=ALU.add))
                c.add(v.tensor_tensor(out=b2, in0=st6[:, :, 1], in1=st6[:, :, 4], op=ALU.subtract))
                c.link(v.tensor_tensor(out=m2, in0=st6[:, :, 2], in1=st6[:, :, 5], op=ALU.add))
                c.add(v.tensor_scalar(mean, a, 0.5, None, ALU.mult))
                c.link(v.tensor_tensor(out=b2, in0=b2, in1=b2, op=ALU.mult))
                c.link(v.scalar_tensor_tensor(out=m2, in0=b2, scalar=D / 4.0, in1=m2, op0=ALU.mult, op1=ALU.add))
                v.tensor_scalar(var, m2, 1.0 / D, LN_EPS, ALU.mult, ALU.add).then_inc(var_ready, 1)

            def inverse_root(r, root, value, t):
                c.link(v.reciprocal(r, root))
                c.link(v.tensor_tensor(out=t, in0=r, in1=r, op=ALU.mult))
                c.link(v.tensor_tensor(out=t, in0=t, in1=value, op=ALU.mult))
                c.link(v.tensor_scalar(t, t, -0.5, 1.5, ALU.mult, ALU.add))
                c.link(v.tensor_tensor(out=r, in0=r, in1=t, op=ALU.mult))

            def rstds(k0, k1):
                mean, rstd, shift, var, root, t = (ln[:, k * NT + k0:k * NT + k1] for k in (0, 1, 2, 3, 4, 5))
                inverse_root(rstd, root, var, t)
                v.scalar_tensor_tensor(out=shift, in0=mean, scalar=-1.0, in1=rstd, op0=ALU.mult, op1=ALU.mult)\
                    .then_inc(rstd_ready, 1)

            def normalise(l):
                for k in range(LOADS):
                    dve.wait_ge(sqrt_ready, (LOADS + 1) * l + k + 1)
                    rstds(k * TPL, (k + 1) * TPL)
                    dve.wait_ge(rstd_ready, (LOADS + 1) * l + k + 1)
                    for t in range(k * TPL, (k + 1) * TPL, 2):
                        v.tensor_scalar(xn[:, t * ROW:t * ROW + D], x[:, t * D:(t + 1) * D], ln[:, t:t + 1],
                                        ln[:, NT + t:NT + t + 1], ALU.subtract, ALU.mult).then_inc(xn_dve, 1)

            def route(l):
                eq_, cand, oh1, L2, oh2, tot, scan, dest = rt

                def per_tile(a):
                    return a[:].unsqueeze(2).to_broadcast([P, NT, E])

                revb = rev[:].unsqueeze(1).to_broadcast([P, NT, E])
                for scores, best, oh, r in ((lg[:], rs[0], oh1, rs[1]), (L2, rs[2], oh2, rs[3])):
                    c.link(v.tensor_reduce(out=best[:], in_=three(scores), axis=AX.X, op=ALU.max))
                    c.link(v.tensor_tensor(out=three(eq_), in0=three(scores), in1=per_tile(best), op=ALU.is_equal))
                    c.link(v.tensor_tensor(out=three(cand), in0=three(eq_), in1=revb, op=ALU.mult))
                    c.link(v.tensor_reduce(out=r[:], in_=three(cand), axis=AX.X, op=ALU.max))
                    c.link(v.tensor_tensor(out=three(oh), in0=three(cand), in1=per_tile(r), op=ALU.is_equal))
                    if oh is oh1:
                        c.link(v.scalar_tensor_tensor(out=L2, in0=oh1, scalar=-BIG, in1=lg[:], op0=ALU.mult, op1=ALU.add))
                v.tensor_tensor(out=m16[:].rearrange("p (e t) -> p t e", e=E), in0=three(oh1), in1=three(oh2),
                                op=ALU.add).then_inc(picks_ready, 1)
                v.tensor_tensor(out=rs[4][:], in0=rs[2][:], in1=rs[0][:], op=ALU.subtract).then_inc(gap_ready, 1)
                dve.wait_ge(ranks_psum, l + 1)
                c.link(v.tensor_copy(tot, bank[5][:, 256:512]))
                c.link(v.tensor_tensor_scan(out=scan, data0=ones[:], data1=tot, initial=0.0, op0=ALU.mult, op1=ALU.add))
                ends = scan.rearrange("p (e t) -> p e t", e=E)
                c.link(v.tensor_copy(r9[:, 1:E + 1], ends[:, :, NT - 1]))
                c.link(v.tensor_tensor(out=r8[0][:], in0=r9[:, 1:E + 1], in1=r9[:, 0:E], op=ALU.subtract))
                c.link(v.tensor_scalar(r8i[0][:], r8[0][:], float(P - 1), None, ALU.add))
                sh = P.bit_length() - 1
                c.link(v.tensor_scalar(r8i[1][:], r8i[0][:], sh, sh, ALU.logical_shift_right, ALU.logical_shift_left))
                c.link(v.tensor_copy(r8[1][:], r8i[1][:]))
                c.link(v.tensor_tensor_scan(out=r8[2][:], data0=ones[:, 0:E], data1=r8[1][:], initial=0.0,
                                            op0=ALU.mult, op1=ALU.add))
                c.link(v.tensor_tensor(out=r8[3][:], in0=r8[2][:], in1=r8[1][:], op=ALU.subtract))
                c.link(v.tensor_tensor(out=r8[4][:], in0=r8[3][:], in1=r9[:, 0:E], op=ALU.subtract))
                c.link(v.tensor_tensor(out=scan, in0=scan, in1=tot, op=ALU.subtract))
                c.link(v.tensor_tensor(out=scan, in0=scan, in1=bank[5][:, 0:256], op=ALU.add))
                c.link(v.tensor_tensor(out=dest.rearrange("p (e t) -> p e t", e=E), in0=ends,
                                       in1=r8[4][:].unsqueeze(2).to_broadcast([P, E, NT]), op=ALU.add))
                for k, oh in enumerate((oh1, oh2)):
                    c.link(v.tensor_tensor(out=three(cand), in0=three(oh),
                                           in1=dest.rearrange("p (e t) -> p t e", e=E), op=ALU.mult))
                    c.link(v.tensor_reduce(out=rs[7][:], in_=three(cand), axis=AX.X, op=ALU.add))
                    c.link(v.tensor_copy(dst[l][k][:], rs[7][:]))
                cmpb = sto[0:1, :]
                c.link(v.tensor_tensor(out=three(cmpb), in0=blk_start[:].unsqueeze(2).to_broadcast([1, NBLK, E]),
                                       in1=r8[2][0:1, :].unsqueeze(1).to_broadcast([1, NBLK, E]), op=ALU.is_ge))
                c.link(v.tensor_reduce(out=bexf[:], in_=three(cmpb), axis=AX.X, op=ALU.add))
                v.tensor_scalar(bex[l][:], bexf[:], float(E - 1), None, ALU.min).then_inc(dest_ready, 1)
                dve.wait_ge(gap_exp, l + 1)
                c.link(v.tensor_scalar(rs[6][:], rs[5][:], 1.0, None, ALU.add))
                c.link(v.reciprocal(wgt[0][:], rs[6][:]))
                v.tensor_tensor(out=wgt[1][:], in0=rs[5][:], in1=wgt[0][:], op=ALU.mult).then_inc(weights_ready, 1)

            for k in range(LOADS):
                dve.wait_ge(x_in[k], 16)
                for t in range(k * TPL, (k + 1) * TPL):
                    c.add(v.bn_stats(st[:, t * 6:(t + 1) * 6], x[:, t * D:(t + 1) * D]))
                c.wait()
                variances(st, k * TPL, (k + 1) * TPL)
            normalise(0)
            dve.wait_ge(scored, B)
            dve.wait_ge(consts_ready, 1)
            c.link(v.tensor_copy(lg[:], bank[4][:, 0:NT * E]))
            route(0)

            dve.wait_ge(small_in, NSMALL)

            def bias(u):
                dve.wait_ge(qkv_psum, u + 1)
                pair = (0, 2, 6)[u % 3]
                v.tensor_tensor(out=big[:, 2 * u * 3 * D:(2 * u + 2) * 3 * D].rearrange("p (t c) -> p t c", t=2),
                                in0=ps[:, pair * 512:(pair + 2) * 512].rearrange("p (t c) -> p t c", t=2)[:, :, 0:3 * D],
                                in1=bqkvb[:].unsqueeze(1).to_broadcast([P, 2, 3 * D]), op=ALU.add).then_inc(qkv_biased, 1)

            bias(0)
            for u in range(NT // 2):
                if u + 1 < NT // 2:
                    bias(u + 1)
                qk = big[:, 2 * u * 3 * D:(2 * u + 2) * 3 * D].rearrange("p (t c) -> p t c", t=2)[:, :, 0:2 * D]
                dve.wait_ge(feat_exp, u + 1)
                c.link(v.tensor_scalar(qk, qk, FEAT_EPS, FEAT_EPS, ALU.add, ALU.max))
                v.scalar_tensor_tensor(out=qk, in0=ex[u % 2].rearrange("p (t c) -> p t c", t=2), scalar=1.0, in1=qk,
                                       op0=ALU.min, op1=ALU.add).then_inc(feat_ready, 1)
            dve.wait_ge(feat_ready, NT // 2)

            def heads(a, n=HE):
                return a.rearrange("p (h c) -> p h c", c=n)

            def outer(t):
                k_, v_ = (big[:, (3 * t + i) * D:(3 * t + i + 1) * D] for i in (1, 2))
                after(dve, tri_psum, t - 1)
                v.tensor_tensor(out=kvx[t % 2].rearrange("p (h f e) -> p h f e", h=H, f=HE),
                                in0=heads(v_).unsqueeze(3).to_broadcast([P, H, HE, HE]),
                                in1=heads(k_).unsqueeze(2).to_broadcast([P, H, HE, HE]), op=ALU.mult).then_inc(kvx_ready, 1)

            def query(t):
                j, pair = t % TPS, 2 * (t % 2)
                q_ = big[:, 3 * t * D:(3 * t + 1) * D]
                dve.wait_ge(tri_psum, t + 1)
                v.tensor_tensor(out=pr[t % 2].rearrange("p (h f e) -> p h f e", h=H, f=HE),
                                in0=ps[:, pair * 512:(pair + 2) * 512].rearrange("p (h f e) -> p h f e", h=H, f=HE),
                                in1=heads(q_).unsqueeze(2).to_broadcast([P, H, HE, HE]), op=ALU.mult).then_inc(prod_ready, 1)
                dve.wait_ge(prod_ready, t + 1)
                c.add(v.tensor_reduce(out=red[:, j * D:(j + 1) * D], in_=heads(pr[t % 2]), axis=AX.X, op=ALU.add))

            def mask(t):
                g, j = t // TPS, t % TPS
                dve.wait_ge(state_psum, g * (TPS - 1) + j + 1)
                if j == 0:
                    v.tensor_tensor(out=stt[t % 2], in0=bank[5][:, 0:P + H], in1=smask[:], op=ALU.mult)\
                        .then_inc(state_ready, 1)
                else:
                    c.link(v.tensor_tensor(out=stt[t % 2], in0=bank[5][:, 0:P + H], in1=smask[:], op=ALU.mult))
                    v.tensor_tensor(out=stt[t % 2], in0=stt[t % 2], in1=stt[(t - 1) % 2], op=ALU.add)\
                        .then_inc(state_ready, 1)

            def divide(g):
                dve.wait_ge(inter_psum, g + 1)
                c.add(v.tensor_tensor(out=red, in0=red, in1=bank[7], op=ALU.add))
                v.tensor_tensor(out=sden, in0=dred, in1=bank[5][:, 256:256 + TPS * H], op=ALU.add).then_inc(sums_ready, 1)
                dve.wait_ge(sums_ready, g + 1)
                c.link(v.tensor_scalar(sden, sden, FEAT_EPS * HE ** 0.5, None, ALU.add))
                c.link(v.reciprocal(rden, sden))
                after(dve, aT_psum, g)
                v.tensor_tensor(out=heads(att), in0=heads(red), in1=rden.unsqueeze(2).to_broadcast([P, TPS * H, HE]),
                                op=ALU.mult).then_inc(att_ready, 1)

            def stats(g):
                dve.wait_ge(o_ready, g + 1)
                for t in range(g * TPS, (g + 1) * TPS):
                    c.add(v.bn_stats(sto[:, t * 6:(t + 1) * 6], attn_o[:, t * D:(t + 1) * D]))

            for g in range(B):
                t = g * TPS
                outer(t)
                outer(t + 1)
                if g:
                    divide(g - 1)
                query(t)
                outer(t + 2)
                mask(t)
                query(t + 1)
                outer(t + 3)
                mask(t + 1)
                if g:
                    stats(g - 1)
                query(t + 2)
                mask(t + 2)
                query(t + 3)
                qs = big[:, 3 * t * D:3 * (t + TPS) * D].rearrange("p (t c) -> p t c", t=TPS)[:, :, 0:D]
                v.tensor_tensor(out=kq.rearrange("p (t c) -> p t c", t=TPS), in0=bank[6].rearrange("p (t c) -> p t c", t=TPS),
                                in1=qs, op=ALU.mult).then_inc(kq_ready, 1)
                dve.wait_ge(kq_ready, g + 1)
                c.link(v.tensor_reduce(out=dred, in_=heads(kq), axis=AX.X, op=ALU.add))
            divide(B - 1)
            c.add(v.tensor_scalar(bzh2[:, 0:2], bzh[:, 0:2], -1.0, None, ALU.mult))
            c.add(v.tensor_scalar(bzh2[:, 2:4], bzh[:, 2:4], 0.5, None, ALU.add))
            c.add(v.reciprocal(rtemp[:], tempb[:]))
            simsq = tmp[0:E, 0:D]
            c.link(v.tensor_tensor(out=simsq, in0=sim[:], in1=sim[:], op=ALU.mult))
            c.link(v.tensor_reduce(out=simn[:, 3:4], in_=simsq, axis=AX.X, op=ALU.add))
            v.tensor_scalar(simn[:, 0:1], simn[:, 3:4], NORM_EPS * NORM_EPS, None, ALU.max).then_inc(sim_sq, 1)
            dve.wait_ge(sim_root, 1)
            inverse_root(simn[:, 2:3], simn[:, 1:2], simn[:, 0:1], simn[:, 3:4])
            v.tensor_scalar(sim[:], sim[:], simn[:, 2:3], None, ALU.mult).then_inc(simn_ready, 1)
            stats(B - 1)
            c.wait()
            variances(sto, 0, NT)
            dve.wait_ge(simT_psum, 1)
            v.tensor_copy(simT[:], bank[7][:, 0:E]).then_inc(simT_ready, 1)
            dve.wait_ge(sqrt_ready, LOADS + 1)
            rstds(0, NT)

            def ffn(l):
                first = l * NBLK
                e = {}

                def hidden(n):
                    if l == 0:
                        dve.wait_ge(up_psum, n + 1)
                        dve.wait_ge(act_ready, n + 1)
                        after(dve, hT_psum, n - 1)
                        v.tensor_tensor(out=fh[n % 2], in0=bank[2 + n % 2], in1=fa[n % 2], op=ALU.mult)\
                            .then_inc(h_ready, 1)
                    else:
                        e[n] = dve.value_load(bex[l][0:1, n - first:n - first + 1], min_val=0, max_val=E - 1)
                        dve.wait_ge(gate_psum, n + 1)
                        after(dve, h_ready, n - 1)
                        v.tensor_tensor(out=fa[n % 2], in0=bank[n % 2], in1=b1b[:, bass.ds(e[n] * F, F)], op=ALU.add)\
                            .then_inc(pre_ready, 1)

                def evict_h(n):
                    dve.wait_ge(hT_psum, n + 1)
                    after(dve, y_psum, n - 1)
                    v.tensor_copy(hT[n % 2], bank[5]).then_inc(hT_ready, 1)

                def evict_y(n):
                    dve.wait_ge(y_psum, n + 1)
                    if n >= NYB:
                        dve.wait_ge(y_out[n % NYB], 16 * (n // NYB))
                    src = bank[7][:, (n % 2) * P:(n % 2 + 1) * P]
                    if l:
                        c.link(v.tensor_tensor(out=yb[n % NYB], in0=src, in1=b2b[:, bass.ds(e.pop(n) * D, D)], op=ALU.add))
                        src = yb[n % NYB]
                    v.tensor_scalar(yb[n % NYB], src, xg[n % NXG][:, WGT:WGT + 1], None, ALU.mult).then_inc(y_ready, 1)

                for b in range(NBLK + 2):
                    n = first + b
                    if b < NBLK:
                        hidden(n)
                    if b >= 2:
                        evict_y(n - 2)
                    if 1 <= b <= NBLK:
                        evict_h(n - 1)

            ffn(0)

            dve.wait_ge(attn_added, B)
            for k in range(LOADS):
                dve.wait_ge(y_in[0][k], 32)
                xk = x[:, k * TPL * D:(k + 1) * TPL * D]
                c.link(v.tensor_tensor(out=xk, in0=xk, in1=y[0][:, k * TPL * D:(k + 1) * TPL * D], op=ALU.add))
                v.tensor_tensor(out=xk, in0=xk, in1=y[1][:, k * TPL * D:(k + 1) * TPL * D], op=ALU.add).then_inc(x_added, 1)
                dve.wait_ge(x_added, k + 1)
                for t in range(k * TPL, (k + 1) * TPL):
                    c.add(v.bn_stats(st[:, t * 6:(t + 1) * 6], x[:, t * D:(t + 1) * D]))
                c.wait()
                variances(st, k * TPL, (k + 1) * TPL)
            for p in range(2):
                dve.wait_ge(listed[p], 16 * NT)
            normalise(1)
            dve.wait_ge(scored, 2 * B)
            v.tensor_scalar(rs[0][:], bank[6][:, 0:NT], NORM_EPS * NORM_EPS, None, ALU.max).then_inc(norms_ready, 1)
            dve.wait_ge(norms_ready, 1)
            dve.wait_ge(sqrt_ready, 2 * LOADS + 2)
            inverse_root(rs[1][:], rs[2][:], rs[0][:], rs[3][:])
            c.link(v.tensor_scalar(rs[3][:], rs[1][:], rtemp[:], None, ALU.mult))
            c.link(v.tensor_tensor(out=three(lg[:]), in0=three(bank[4][:, 0:NT * E]),
                                   in1=rs[3][:].unsqueeze(2).to_broadcast([P, NT, E]), op=ALU.mult))
            route(1)

            def gru_add(g):
                dve.wait_ge(gruT_psum, g + 1)
                v.tensor_tensor(out=x[:, g * S:(g + 1) * S], in0=x[:, g * S:(g + 1) * S], in1=bank[7], op=ALU.add)\
                    .then_inc(gruT_added, 1)

            for n, (l, g) in enumerate(order):
                s = g % 2
                h = (gh1, gh2)[l][s]
                dve.wait_ge(gru_act, n + 1)
                c.link(v.scalar_tensor_tensor(out=gs[s], in0=bank[2 * l + 1], scalar=bzh2[:, 2 + l:3 + l], in1=gs[s],
                                              op0=ALU.add, op1=ALU.max))
                c.link(v.tensor_tensor(out=gz[s], in0=gz[s], in1=gs[s], op=ALU.mult))
                if l == 1:
                    after(dve, gruT_psum, g - 1)
                else:
                    after(dve, gru_psum, order.index((1, g - 2)) + 1 if g >= 2 else 0)
                v.tensor_tensor_scan(out=h, data0=ga[s], data1=gz[s], initial=0.5, op0=ALU.mult, op1=ALU.add)\
                    .then_inc(gru_scan, 1)
                if l == 1 and g:
                    gru_add(g - 1)
            gru_add(B - 1)
            dve.wait_ge(w2_in, 16 * 3 * E)
            ffn(1)
            for k in range(LOADS):
                dve.wait_ge(y_in[1][k], 32)
                xk = x[:, k * TPL * D:(k + 1) * TPL * D]
                c.link(v.tensor_tensor(out=xk, in0=xk, in1=y[0][:, k * TPL * D:(k + 1) * TPL * D], op=ALU.add))
                v.tensor_tensor(out=xk, in0=xk, in1=y[1][:, k * TPL * D:(k + 1) * TPL * D], op=ALU.add).then_inc(out_ready, 1)


def kernel(**inputs):
    import numpy as _np
    import concourse.bacc as _bacc
    from concourse import mybir as _mybir
    from concourse.bass_utils import run_bass_kernel_spmd as _run

    a = {k: _np.asarray(v) for k, v in inputs.items()}
    wqkv = a["L0_attn_Wqkv"]
    laid = {
        "x": a["L0_attn_x"],
        "wqkv": wqkv.T,
        "bqkv": a["L0_attn_bqkv"],
        "wout": a["L0_attn_Wout"].T,
        "bout": a["L0_attn_bout"].reshape(1, 128), "gamma": a["L0_attn_gamma"], "beta": a["L0_attn_beta"],
        "gatew": a["L0_ffn_gate_w"].T,
        "gu": a["L0_ffn_gate_up_w"].transpose(2, 0, 1).reshape(128, -1),
        "dw": a["L0_ffn_down_w"].reshape(8, 128, 4, 128).transpose(3, 0, 2, 1).reshape(128, -1),
        "wz": a["L1_attn_Wz"].transpose(2, 0, 1).reshape(128, -1), "bz": a["L1_attn_bz"].T,
        "wh": a["L1_attn_Wh"].transpose(2, 0, 1).reshape(128, -1), "bh": a["L1_attn_bh"].T,
        "wp": a["L1_ffn_Wp"].T, "sim": a["L1_ffn_sim_matrix"], "temp": a["L1_ffn_temperature"].reshape(1),
        "w1": a["L1_ffn_W1"].transpose(1, 0, 2).reshape(128, -1), "b1": a["L1_ffn_b1"].reshape(-1),
        "w2": a["L1_ffn_W2"].reshape(8, 4, 128, 128).transpose(2, 0, 1, 3).reshape(128, -1),
        "b2": a["L1_ffn_b2"].reshape(-1),
    }
    nc = _bacc.Bacc("TRN2", target_bir_lowering=False, num_devices=1)
    arrays, args = {}, []
    for name, v in laid.items():
        v = _np.ascontiguousarray(v)
        arrays[f"in_{name}"] = v
        args.append(nc.dram_tensor(f"in_{name}", v.shape, _mybir.dt.from_np(v.dtype), kind="ExternalInput").ap())
    f32 = _mybir.dt.float32
    for l in range(2):
        args.append(nc.dram_tensor(f"sorted_tokens{l}", (NBLK * P, ROW), f32, kind="Internal").ap())
    args.append(nc.dram_tensor("results", ((2 * NT + NBLK) * P, D), f32, kind="Internal").ap())
    args.append(nc.dram_tensor("out", (B, S, D), f32, kind="ExternalOutput").ap())
    build(nc, *args)
    return _run(nc, [arrays], core_ids=[0]).results[0]["out"]
```

```python
import concourse.bass as bass
from concourse import mybir
from concourse.alu_op_type import AluOpType as ALU
from contextlib import ExitStack

P = 128
B, S, D = 8, 512, 128
NT = B * S // P
TPS = S // P
HALF = NT // 2
H, HE = 16, 8
E, F = 8, 512
FC = F // P
NBLK = 2 * NT + E - 1
ROW = D + 2
TAG, WGT = D, D + 1
FEAT_EPS = 1e-4
LN_EPS = 1e-5
NORM_EPS = 1e-12
LOADS, STORES = 4, 8
TPL = NT // LOADS
NXG, NXT, NYB = 8, 3, 4
BIG = 3.0e38
EARLY, SHARE = 3, 8
POOL_GROUPS = 3
FEAT_POOL = 12
ROUTE_STEPS = 40
O_FROM = B + 4
NEX, LAG = 4, 4
QKV_BANKS = (2, 6)


class Chain:

    def __init__(self, engine, sem):
        self.engine, self.sem, self.n = engine, sem, 0

    def add(self, ins):
        ins.then_inc(self.sem, 1)
        self.n += 1

    def wait(self):
        self.engine.wait_ge(self.sem, self.n)

    def link(self, ins):
        self.add(ins)
        self.wait()


def after(engine, sem, n):
    if n > 0:
        engine.wait_ge(sem, n)


def build(nc, x_d, wqkv_d, bqkv_d, wout_d, bout_d, gamma_d, beta_d, gatew_d, gu_d, dw_d,
          wz_d, bz_d, wh_d, bh_d, wp_d, sim_d, temp_d, w1_d, b1_d, w2_d, b2_d, list0_d, list1_d, res_d, out_d):
    fp32, bf16 = mybir.dt.float32, mybir.dt.bfloat16
    i32, u32 = mybir.dt.int32, mybir.dt.uint32
    ACT = mybir.ActivationFunctionType
    AX = mybir.AxisListType

    ctx = ExitStack()
    with ctx:
        def sb(name, shape, dt=fp32):
            return ctx.enter_context(nc.sbuf_tensor(name, shape, dt))

        def sem(name):
            return ctx.enter_context(nc.semaphore(name))

        def sems(name, n=2):
            return [sem(f"{name}{k}") for k in range(n)]

        x = sb("x", [P, NT * D])
        xn = sb("xn", [P, NT * ROW])
        xnT = sb("xnT", [P, NT * P])
        attn_o = xnT
        gu = sb("gu", [P, E * 2 * F])
        dw = sb("dw", [P, E * FC * D])
        y = [gu[:, k * NT * D:(k + 1) * NT * D] for k in range(2)]
        big = sb("big", [P, 3 * NT * D])
        w1 = big[:, 0:E * F]
        w2 = big[:, E * F:2 * E * F]
        b1b = big[:, 2 * E * F:3 * E * F]
        b2b = sb("b2b", [P, E * D])
        scr = sb("scr", [P, 6144])
        qTb = sb("qTb", [P, 2 * S])
        tmp = sb("tmp", [P, 2048])
        ident = sb("ident", [P, P])
        ones = sb("ones", [P, NT * E])
        tri = sb("tri", [P, P])
        smask = sb("smask", [P, P + H])
        upper16 = sb("upper16", [P, P], bf16)
        ones16 = sb("ones16", [P, P], bf16)
        rev = sb("rev", [P, E])
        blk_start = sb("blk_start", [1, NBLK])
        wqkv = sb("wqkv", [P, 3 * D])
        wout = sb("wout", [P, D])
        gatew = sb("gatew", [P, E])
        wz = sb("wz", [P, 2 * D])
        wh = sb("wh", [P, 2 * D])
        wps = sb("wps", [P, D + E])
        wpT = sb("wpT", [P, D])
        bzh = sb("bzh", [P, 4])
        bzh2 = sb("bzh2", [P, 4])
        bqkvb = sb("bqkvb", [P, 3 * D])
        boutr = sb("boutr", [1, D])
        gammab = sb("gammab", [P, D])
        betab = sb("betab", [P, D])
        tempb = sb("tempb", [P, 1])
        rtemp = sb("rtemp", [P, 1])
        idle = sb("idle", [P, 1])
        sim = sb("sim", [E, D])
        simn = sb("simn", [E, 4])
        simT = sb("simT", [P, E])
        state = sb("state", [P, (TPS - 1) * (P + H)])
        st = sb("st", [P, NT * 6])
        sto = sb("sto", [P, NBLK * E])
        ln = sb("ln", [P, 8 * NT])
        lg = sb("lg", [P, NT * E])
        rs = [sb(f"rs{k}", [P, NT]) for k in range(8)]
        r9 = sb("r9", [P, E + 1])
        r8 = [sb(f"r8_{k}", [P, E]) for k in range(5)]
        r8i = [sb(f"r8i_{k}", [P, E], i32) for k in range(2)]
        m16 = sb("m16", [P, NT * E], bf16)
        wgt = [sb(f"wgt{k}", [P, NT]) for k in range(2)]
        dst = [[sb(f"dst{l}_{k}", [P, NT], u32) for k in range(2)] for l in range(2)]
        bexf = sb("bexf", [1, NBLK])
        bex = [sb(f"bex{l}", [1, NBLK], i32) for l in range(2)]

        def part(a, at, size, n):
            return [a[:, at + k * size:at + (k + 1) * size] for k in range(n)]

        rt = part(tmp, 0, NT * E, 8)
        ex = part(scr, 2048, S, NEX)
        kvx = part(scr, 0, 1024, 2) + [tmp[:, 1024:2048]]
        pr = part(scr, 2048, 1024, 2)
        red = part(scr, 4096, S, 2)
        att = scr[:, 5120:5632]
        aT = scr[:, 5632:6144]
        kq = tmp[:, 0:S]
        dred, rden = part(lg, 0, TPS * H, 2)
        qT = part(qTb, 0, S, 2)
        stt = part(state, 0, P + H, TPS - 1)
        fa = part(scr, 0, F, 2)
        fh = part(scr, 1024, F, 2)
        hT = part(scr, 2048, F, 2)
        xg = part(scr, 3072, ROW, NXG)
        xgT = part(scr, 3072 + NXG * ROW, P, NXT)
        yb = part(scr, 3072 + NXG * ROW + NXT * P, D, NYB)
        sq = part(scr, 0, S, 2)
        ga, gz, gs, gh1, gh2 = (part(scr, 1024 * k, S, 2) for k in range(5))

        def col(a, k):
            return a.rearrange("p (t r) -> p t r", r=ROW)[:, :, k]

        NG = gu.shape[1] // ROW
        FILL = [(gu[:, 0:NG * ROW], 0, NG), (dw[:, 0:(NBLK - NG) * ROW], NG, NBLK - NG)]

        ps = ctx.enter_context(nc.psum_tensor("ps", [P, 8 * 512], fp32))
        bank = part(ps, 0, 512, 8)

        x_in = sems("x_in", LOADS)
        small_in, gu_in, dw_in, w2_in = sem("small_in"), sem("gu_in"), sem("dw_in"), sem("w2_in")
        list_filled = sems("list_filled")
        pool_step, dve_step = sem("pool_step"), sem("dve_step")
        consts_ready, fill_ready = sem("consts_ready"), sem("fill_ready")
        var_ready, sqrt_ready = sem("var_ready"), sem("sqrt_ready")
        rstd_ready = sem("rstd_ready")
        xn_pool, xn_dve, xn_act = sem("xn_pool"), sem("xn_dve"), sem("xn_act")
        xT_psum, xT_ready, scored = sem("xT_psum"), sem("xT_ready"), sem("scored")
        proj_psum, proj_ready, proj_read = sem("proj_psum"), sem("proj_ready"), sem("proj_read")
        gap_ready, gap_exp, picks_ready = sem("gap_ready"), sem("gap_exp"), sem("picks_ready")
        weights_ready = sem("weights_ready")
        ranks_psum, dest_ready, blocks_ready = sem("ranks_psum"), sem("dest_ready"), sem("blocks_ready")
        feat_max, feat_dve = sem("feat_max"), sem("feat_dve")
        norms_ready, sim_sq, sim_root = sem("norms_ready"), sem("sim_sq"), sem("sim_root")
        listed = [sems(f"listed{l}_", 4) for l in range(2)]
        simn_ready, simT_psum, simT_ready = sem("simn_ready"), sem("simT_psum"), sem("simT_ready")
        qkv_psum, qkv_biased, feat_exp, feat_ready = sem("qkv_psum"), sem("qkv_biased"), sem("feat_exp"), sem("feat_ready")
        kvx_ready, kvx_pool = sem("kvx_ready"), sem("kvx_pool")
        tri_psum, ksum_psum, prod_ready = sem("tri_psum"), sem("ksum_psum"), sem("prod_ready")
        kq_ready, state_psum, state_ready = sem("kq_ready"), sem("state_psum"), sem("state_ready")
        inter_psum, sums_ready, att_ready = sem("inter_psum"), sem("sums_ready"), sem("att_ready")
        qT_psum, qT_ready, aT_psum, aT_ready = sem("qT_psum"), sem("qT_ready"), sem("aT_psum"), sem("aT_ready")
        o_psum, o_ready = sem("o_psum"), sem("o_ready")
        o_normed, attn_added = sem("o_normed"), sem("attn_added")
        xg_in = sems("xg_in", NXG)
        xgT_psum, xgT_ready = sem("xgT_psum"), sem("xgT_ready")
        gate_psum, up_psum, act_ready, pre_ready = sem("gate_psum"), sem("up_psum"), sem("act_ready"), sem("pre_ready")
        h_ready, hT_psum, hT_ready = sem("h_ready"), sem("hT_psum"), sem("hT_ready")
        y_psum, y_ready = sem("y_psum"), sem("y_ready")
        y_out = sems("y_out", NYB)
        y_in = [sems("y_in0_", LOADS), sems("y_in1_", STORES)]
        y_summed, x_added = sem("y_summed"), sem("x_added")
        gru_psum, gru_act, gru_scan = sem("gru_psum"), sem("gru_act"), sem("gru_scan")
        gruT_psum, gruT_added = sem("gruT_psum"), sem("gruT_added")
        out_ready, stored = sem("out_ready"), sem("stored")

        block = ctx.enter_context(nc.Block())

        SMALL = [(wqkv, wqkv_d), (wout, wout_d), (gatew, gatew_d), (wz, wz_d), (wh, wh_d), (wps[:, 0:D], wp_d),
                 (boutr, bout_d), (bzh[:, 0:2], bz_d), (bzh[:, 2:4], bh_d), (sim, sim_d)]
        BCAST = [(bqkvb, bqkv_d), (gammab, gamma_d), (betab, beta_d), (tempb, temp_d), (b2b, b2_d)]
        NSMALL = 16 * (len(SMALL) + len(BCAST))
        x_rows = x_d.rearrange("b (c p) d -> p (b c) d", p=P)
        out_rows = out_d.rearrange("b (c p) d -> p (b c) d", p=P)
        res_rows = res_d[0:2 * NT * P, :].rearrange("(t p) d -> p t d", p=P)
        lists = [list0_d, list1_d]

        def group(a, k, n=TPL):
            return a[:, k * n * D:(k + 1) * n * D].rearrange("p (t d) -> p t d", d=D)

        def heads(a, n=HE):
            return a.rearrange("p (h c) -> p h c", c=n)

        def qkv(t, k):
            return big[:, (3 * t + k) * D:(3 * t + k + 1) * D]

        def by_pool(t):
            return t >= EARLY and t % SHARE != SHARE - 1

        def outers(t):
            return sum(by_pool(i) == by_pool(t) for i in range(t + 1))

        def outer(engine, t):
            after(engine, tri_psum, t - 2)
            return engine.tensor_tensor(out=kvx[t % 3].rearrange("p (h f e) -> p h f e", h=H, f=HE),
                                        in0=heads(qkv(t, 2)).unsqueeze(3).to_broadcast([P, H, HE, HE]),
                                        in1=heads(qkv(t, 1)).unsqueeze(2).to_broadcast([P, H, HE, HE]), op=ALU.mult)

        order = [(0, 0), (0, 1)]
        for g in range(B):
            order.append((1, g))
            if g + 2 < B:
                order.append((0, g + 2))

        @block.sync
        def _(sp):
            for k in range(LOADS):
                sp.dma_start(group(x, k), x_rows[:, k * TPL:(k + 1) * TPL, :]).then_inc(x_in[k], 16)

            sp.wait_ge(small_in, NSMALL)
            sp.wait_ge(fill_ready, len(FILL))
            for l in range(2):
                for src, c0, n in FILL:
                    sp.dma_start(lists[l].rearrange("(p c) r -> p (c r)", p=P)[:, c0 * ROW:(c0 + n) * ROW], src)\
                        .then_inc(list_filled[l], 16)
            for l in range(2):
                sp.wait_ge(list_filled[l], 16 * len(FILL))
            sp.dma_start(gu[:], gu_d).then_inc(gu_in, 16)
            sp.dma_start(dw[:], dw_d).then_inc(dw_in, 16)

            def load_blocks(l):
                for part_listed in listed[l]:
                    sp.wait_ge(part_listed, 16 * HALF)
                for b in range(NBLK):
                    n = l * NBLK + b
                    if b >= NXG:
                        sp.wait_ge(y_out[(n - NXG) % NYB], 16 * ((n - NXG) // NYB + 1))
                    sp.dma_start(xg[n % NXG], lists[l][b * P:(b + 1) * P, :]).then_inc(xg_in[n % NXG], 16)
                    if l == 0 and 8 <= b < 8 + E:
                        e = b - 8
                        for to, src in ((w1, w1_d), (w2, w2_d)):
                            sp.dma_start(to[:, e * F:(e + 1) * F], src[:, e * F:(e + 1) * F]).then_inc(w2_in, 16)
                        sp.dma_start(b1b[:, e * F:(e + 1) * F], b1_d[e * F:(e + 1) * F].partition_broadcast(P))\
                            .then_inc(w2_in, 16)

            def load_results(l):
                n = (l + 1) * NBLK
                for s in range(NYB):
                    sp.wait_ge(y_out[s], 16 * ((n - s + NYB - 1) // NYB))
                if l == 0:
                    sp.wait_ge(y_psum, n)
                else:
                    sp.wait_ge(x_added, LOADS)
                groups = (LOADS, STORES)[l]
                m = NT // groups
                for k in range(groups):
                    for p in range(2):
                        sp.dma_start(group(y[p], k, m), res_rows[:, p * NT + k * m:p * NT + (k + 1) * m, :])\
                            .then_inc(y_in[l][k], 16)

            sp.wait_ge(kq_ready, B)
            load_blocks(0)
            load_results(0)
            sp.wait_ge(gruT_psum, B)
            load_blocks(1)
            load_results(1)
            m = NT // STORES
            for k in range(STORES):
                sp.wait_ge(out_ready, k + 1)
                sp.dma_start(out_rows[:, k * m:(k + 1) * m, :], group(x, k, m)).then_inc(stored, 16)
            sp.wait_ge(stored, 16 * STORES)

        @block.gpsimd
        def _(pool):
            c = Chain(pool, pool_step)
            for src, c0, n in FILL:
                c.link(pool.memset(src, 0.0))
                pool.iota(col(src.bitcast(i32), TAG), [[1, n]], base=2 * NT * P + c0, channel_multiplier=NBLK)\
                    .then_inc(fill_ready, 1)
            for to, v in ((idle, 0.0), (ident, 0.0), (ones, 1.0), (tri, 1.0), (smask, 1.0), (upper16, 1.0), (ones16, 1.0)):
                c.add(pool.memset(to[:], v))
            c.wait()

            def select(t, pattern, base, mult, op, value):
                c.add(pool.affine_select(out=t, in_=t, compare_op=op, fill=value, base=base, pattern=pattern,
                                         channel_multiplier=mult))

            select(ident[:], [[-1, P]], 0, 1, ALU.not_equal, 1.0)
            select(tri[:], [[1, P]], 0, -1, ALU.is_ge, 0.0)
            select(upper16[:], [[1, P]], -1, -1, ALU.is_ge, 0.0)
            blocks = smask[:, 0:P].rearrange("p (h c) -> p h c", c=HE)
            heads = smask[:, P:P + H].unsqueeze(2)
            for v, w in ((blocks, HE), (heads, 1)):
                select(v, [[-HE, H], [0, w]], 0, 1, ALU.is_ge, 0.0)
            c.wait()
            for v, w in ((blocks, HE), (heads, 1)):
                select(v, [[HE, H], [0, w]], HE - 1, -1, ALU.is_ge, 0.0)
            c.add(pool.iota(blk_start[:], [[P, NBLK]], base=0, channel_multiplier=0,
                            allow_small_or_imprecise_dtypes=True))
            c.add(pool.iota(rev[:], [[-1, E]], base=E, channel_multiplier=0, allow_small_or_imprecise_dtypes=True))
            c.wait()
            pool.memset(r9[:, 0:1], 0.0).then_inc(consts_ready, 1)

            def normalise(l):
                for k in range(POOL_GROUPS):
                    pool.wait_ge(rstd_ready, (LOADS + 1) * l + k + 1)
                    for t in range(k * TPL, (k + 1) * TPL, 2):
                        pool.tensor_scalar(xn[:, t * ROW:t * ROW + D], x[:, t * D:(t + 1) * D], ln[:, t:t + 1],
                                           ln[:, NT + t:NT + t + 1], ALU.subtract, ALU.mult).then_inc(xn_pool, 1)

            def tag(l, k, half):
                ts = slice(half * HALF, (half + 1) * HALF)
                if k:
                    pool.wait_ge(listed[l][half], 16 * HALF)
                elif l:
                    pool.wait_ge(listed[0][2 + half], 16 * HALF)
                c.link(pool.iota(col(xn[:].bitcast(i32), TAG)[:, ts], [[P, HALF]], base=(k * NT + half * HALF) * P,
                                 channel_multiplier=1))
                if k + half == 0:
                    pool.wait_ge(weights_ready, l + 1)
                c.link(pool.tensor_copy(col(xn[:], WGT)[:, ts], wgt[k][:, ts]))

            def scatter(l, i):
                k, t = i // NT, i % NT
                if t % HALF == 0:
                    tag(l, k, t // HALF)
                if t == 0:
                    pool.wait_ge(dest_ready, 2 * l + k + 1)
                if i == 0:
                    pool.wait_ge(xn_pool, (l + 1) * POOL_GROUPS * TPL // 2)
                    pool.wait_ge(xn_dve, (l + 1) * (LOADS - POOL_GROUPS) * TPL // 2)
                    pool.wait_ge(xn_act, (l + 1) * NT // 2)
                    pool.wait_ge(list_filled[l], 16 * len(FILL))
                pool.indirect_dma_start(lists[l], bass.IndirectOffsetOnAxis(ap=dst[l][k][:, t:t + 1], axis=0),
                                        xn[:, t * ROW:(t + 1) * ROW], None).then_inc(listed[l][i // HALF], 16)

            def put_result(n):
                pool.wait_ge(y_ready, n + 1)
                pool.indirect_dma_start(res_d, bass.IndirectOffsetOnAxis(ap=xg[n % NXG][:, TAG:TAG + 1].bitcast(u32), axis=0),
                                        yb[n % NYB], None).then_inc(y_out[n % NYB], 16)

            normalise(0)
            for u in range(FEAT_POOL):
                qk = big[:, 2 * u * 3 * D:(2 * u + 2) * 3 * D].rearrange("p (t c) -> p t c", t=2)[:, :, 0:2 * D]
                pool.wait_ge(feat_max, u + 1)
                c.link(pool.tensor_scalar(ex[u % NEX], ex[u % NEX], 1.0, None, ALU.min))
                pool.tensor_tensor(out=qk, in0=ex[u % NEX].rearrange("p (t c) -> p t c", t=2), in1=qk, op=ALU.add)\
                    .then_inc(feat_ready, 1)
            pool.wait_ge(feat_ready, FEAT_POOL)
            pool.wait_ge(feat_dve, NT // 2 - FEAT_POOL)
            pool.wait_ge(blocks_ready, 1)
            for t in range(NT):
                if by_pool(t):
                    outer(pool, t).then_inc(kvx_pool, 1)
                scatter(0, 2 * t)
                scatter(0, 2 * t + 1)
            beta4 = betab[:].unsqueeze(1).to_broadcast([P, TPS, D])
            gamma4 = gammab[:].unsqueeze(1).to_broadcast([P, TPS, D])
            for n in range(NBLK):
                put_result(n)
                g = (n - O_FROM) // TPS - 1
                if n % TPS == 0 and 0 <= g < B:
                    c.add(pool.tensor_tensor(out=group(x, g, TPS), in0=group(x, g, TPS), in1=beta4, op=ALU.add))
                if n % TPS == 2 and 0 <= g < B:
                    pool.wait_ge(o_normed, (g + 1) * TPS)
                    o = group(attn_o, g, TPS)
                    c.link(pool.tensor_tensor(out=o, in0=o, in1=gamma4, op=ALU.mult))
                    pool.tensor_tensor(out=group(x, g, TPS), in0=group(x, g, TPS), in1=o, op=ALU.add)\
                        .then_inc(attn_added, 1)

            def sum_results(l):
                groups = (LOADS, STORES)[l]
                m = NT // groups
                for k in range(groups):
                    pool.wait_ge(y_in[l][k], 32)
                    pool.tensor_tensor(out=group(y[0], k, m), in0=group(y[0], k, m), in1=group(y[1], k, m), op=ALU.add)\
                        .then_inc(y_summed, 1)

            sum_results(0)
            for part_listed in listed[0]:
                pool.wait_ge(part_listed, 16 * HALF)
            normalise(1)
            for i in range(2 * NT):
                scatter(1, i)
            for n in range(NBLK, 2 * NBLK):
                put_result(n)
            sum_results(1)

        @block.tensor
        def _(pe):
            mm, xpose = nc.tensor.matmul, nc.tensor.transpose
            pe.wait_ge(consts_ready, 1)
            pe.wait_ge(small_in, NSMALL)

            def cols(j, n=P):
                return slice(j * n, (j + 1) * n)

            def to_channels(l):
                for g in range(B + 1):
                    if g < B:
                        n = l * B + g
                        ahead = POOL_GROUPS * TPL // TPS
                        if g < ahead:
                            pe.wait_ge(xn_pool, (l * ahead + g + 1) * TPS // 2)
                        else:
                            pe.wait_ge(xn_dve, (l * (B - ahead) + g - ahead + 1) * TPS // 2)
                        pe.wait_ge(xn_act, (n + 1) * TPS // 2)
                        after(pe, xT_ready, n - 1)
                        for j in range(TPS):
                            t = g * TPS + j
                            ins = xpose(bank[g % 2][:, cols(j)], xn[:, t * ROW:t * ROW + D], ident[:])
                        ins.then_inc(xT_psum, 1)
                    if g > 0:
                        yield g - 1

            def to_qkv(u):
                after(pe, qkv_biased, u - 1)
                for k in range(2):
                    t = 2 * u + k
                    ins = mm(bank[QKV_BANKS[u % 2] + k][:, 0:3 * D], xnT[:, cols(t)], wqkv[:], start=True, stop=True)
                ins.then_inc(qkv_psum, 1)

            for g in to_channels(0):
                pe.wait_ge(xT_ready, g + 1)
                for j in range(TPS):
                    t = g * TPS + j
                    ins = mm(bank[4][:, cols(t, E)], xnT[:, cols(t)], gatew[:], start=True, stop=True)
                ins.then_inc(scored, 1)
                to_qkv(g)

            def ranks(l):
                pe.wait_ge(picks_ready, l + 1)
                mm(bank[5][:, 0:256], upper16[:], m16[:], start=True, stop=True)
                mm(bank[5][:, 256:512], ones16[:], m16[:], start=True, stop=True).then_inc(ranks_psum, 1)

            for u in range(B, NT // 2):
                if u == B + 4:
                    ranks(0)
                if u == B + 5:
                    pe.wait_ge(simn_ready, 1)
                    xpose(bank[4][:, 0:E], sim[:], ident[0:E, 0:E])
                    xpose(bank[4][:, P:2 * P], wps[:, 0:D], ident[:]).then_inc(simT_psum, 1)
                if u == B + 6:
                    pe.wait_ge(simT_ready, 1)
                    mm(bank[4][:, 0:E], wpT[:], simT[:], start=True, stop=True).then_inc(simT_psum, 1)
                to_qkv(u)
            pe.wait_ge(qkv_biased, NT // 2)

            def running(t):
                pair = 2 * (t % 2)
                if by_pool(t):
                    pe.wait_ge(kvx_pool, outers(t))
                else:
                    pe.wait_ge(kvx_ready, outers(t))
                after(pe, prod_ready, t - 1)
                mm(bank[pair], tri[:], kvx[t % 3][:, 0:512], start=True, stop=True)
                mm(bank[pair + 1], tri[:], kvx[t % 3][:, 512:1024], start=True, stop=True).then_inc(tri_psum, 1)

            def ksums(t):
                if t % TPS == 0:
                    after(pe, kq_ready, t // TPS)
                mm(bank[6][:, cols(t % TPS)], tri[:], qkv(t, 1), start=True, stop=True).then_inc(ksum_psum, 1)

            def update(t):
                g, j = t // TPS, t % TPS
                after(pe, state_ready, g * (TPS - 1) + j)
                mm(bank[5][:, 0:P], qkv(t, 1), qkv(t, 2), start=(j == 0), stop=True, skip_group_check=True)
                mm(bank[5][:, P:P + H], qkv(t, 1), ones[:, 0:H], start=False, stop=True,
                   skip_group_check=True).then_inc(state_psum, 1)

            def across(g):
                pe.wait_ge(state_ready, (g + 1) * (TPS - 1))
                pe.wait_ge(qT_ready, g + 1)
                after(pe, sums_ready, g)
                for j in range(1, TPS):
                    lhs = qT[g % 2][:, cols(j)]
                    mm(bank[7][:, cols(j)], lhs, stt[j - 1][:, 0:P], start=True, stop=True)
                    ins = mm(bank[7][:, cols(j, H)], lhs, stt[j - 1][:, P:P + H], start=True, stop=True)
                ins.then_inc(inter_psum, 1)

            def xpose_out(g):
                pe.wait_ge(att_ready, g + 1)
                pe.wait_ge(qT_ready, g + 1)
                for j in range(TPS):
                    ins = xpose(bank[4][:, cols(j)], att[:, cols(j)], ident[:])
                ins.then_inc(aT_psum, 1)

            def project(g, half):
                pe.wait_ge(aT_ready, g + 1)
                for j in range(2 * half, 2 * half + 2):
                    mm(bank[4][:, cols(j)], ones[0:1, 0:P], boutr[:], start=True, stop=False)
                    ins = mm(bank[4][:, cols(j)], aT[:, cols(j)], wout[:], start=False, stop=True)
                if half:
                    ins.then_inc(o_psum, 1)

            def xpose_q(g):
                if g:
                    pe.wait_ge(o_ready, g)
                else:
                    pe.wait_ge(picks_ready, 1)
                    pe.wait_ge(simT_ready, 2)
                for j in range(TPS):
                    ins = xpose(bank[4][:, cols(j)], qkv(g * TPS + j, 0), ident[:])
                ins.then_inc(qT_psum, 1)

            for g in range(B):
                t = g * TPS
                running(t)
                if g:
                    across(g - 1)
                else:
                    pe.wait_ge(dest_ready, 1)
                update(t)
                ksums(t)
                running(t + 1)
                update(t + 1)
                ksums(t + 1)
                if g:
                    xpose_out(g - 1)
                running(t + 2)
                update(t + 2)
                ksums(t + 2)
                if g:
                    project(g - 1, 0)
                running(t + 3)
                if g:
                    project(g - 1, 1)
                ksums(t + 3)
                xpose_q(g)
            across(B - 1)

            def ffn(l):
                wa, wb, wid = (gu, dw[:], 2 * F) if l == 0 else (w1, w2, F)
                first = l * NBLK

                def load_xpose(n):
                    pe.wait_ge(xg_in[n % NXG], 16 * (n // NXG + 1))
                    after(pe, xgT_ready, n)
                    xpose(bank[6][:, cols(n % NXT)], xg[n % NXG][:, 0:D], ident[:]).then_inc(xgT_psum, 1)

                def expert(n):
                    return pe.value_load(bex[l][0:1, n - first:n - first + 1], min_val=0, max_val=E - 1)

                def up(n, e):
                    pe.wait_ge(xgT_ready, n + 1)
                    after(pe, pre_ready if l else act_ready, n - first - 1)
                    mm(bank[n % 2], xgT[n % NXT], wa[:, bass.ds(e * wid, F)], start=True, stop=True).then_inc(gate_psum, 1)
                    if l == 0:
                        after(pe, h_ready, n - 1)
                        mm(bank[2 + n % 2], xgT[n % NXT], wa[:, bass.ds(e * wid + F, F)], start=True, stop=True)\
                            .then_inc(up_psum, 1)

                def down(n, e):
                    pe.wait_ge(hT_ready, n + 1)
                    after(pe, y_ready, n)
                    for fc in range(FC):
                        ins = mm(bank[7][:, cols(n % 2)], hT[n % 2][:, cols(fc)],
                                 wb[:, bass.ds(e * FC * D + fc * D, D)], start=(fc == 0), stop=(fc == FC - 1))
                    ins.then_inc(y_psum, 1)

                def xpose_h(n):
                    pe.wait_ge(h_ready, n + 1)
                    after(pe, hT_ready, n)
                    for fc in range(FC):
                        ins = xpose(bank[5][:, cols(fc)], fh[n % 2][:, cols(fc)], ident[:])
                    ins.then_inc(hT_psum, 1)

                pe.wait_ge(blocks_ready, l + 1)
                load_xpose(first)
                load_xpose(first + 1)
                e = {0: expert(first)}
                for b in range(NBLK + 2):
                    n = first + b
                    if b < NBLK:
                        up(n, e[b])
                    if b + 2 < NBLK:
                        load_xpose(n + 2)
                    if l == 0 and b == 0:
                        xpose_out(B - 1)
                        pe.wait_ge(state_ready, B * (TPS - 1))
                    if l == 0 and b == 2:
                        pe.wait_ge(sums_ready, B)
                    if b >= 2:
                        down(n - 2, e.pop(b - 2))
                    if 1 <= b <= NBLK:
                        xpose_h(n - 1)
                    if l == 0 and b == 1:
                        project(B - 1, 0)
                        project(B - 1, 1)
                    if b + 1 < NBLK:
                        e[b + 1] = expert(n + 1)

            pe.wait_ge(gu_in, 16)
            pe.wait_ge(dw_in, 16)
            pe.wait_ge(kq_ready, B)
            ffn(0)

            for g in to_channels(1):
                pe.wait_ge(xT_ready, B + g + 1)
                after(pe, proj_ready, g - 1)
                for j in range(TPS):
                    at = (2 + 2 * (g % 2)) * 512 + j * 256
                    ins = mm(ps[:, at:at + D + E], xnT[:, cols(g * TPS + j)], wps[:], start=True, stop=True)
                ins.then_inc(proj_psum, 1)

            def gru(l, g):
                n = 2 * g + l if g else l
                s = l
                after(pe, gru_scan, order.index((l, g - 1)) + 1 if g else 0)
                if l:
                    pe.wait_ge(gru_scan, order.index((0, g)) + 1)
                rhs = xnT[:, cols(g, S)] if l == 0 else gh1[g % 2]
                mm(bank[2 * s], wz[:, cols(l)], rhs, start=True, stop=True)
                mm(bank[2 * s + 1], wh[:, cols(l)], rhs, start=True, stop=True).then_inc(gru_psum, 1)

            def gru_out(g):
                pe.wait_ge(gru_scan, order.index((1, g)) + 1)
                after(pe, gruT_added, g)
                for j in range(TPS):
                    ins = xpose(bank[7][:, cols(j)], gh2[g % 2][:, cols(j)], ident[:])
                ins.then_inc(gruT_psum, 1)

            gru(0, 0)
            ranks(1)
            gru(0, 1)
            for g in range(B):
                gru(1, g)
                if g + 2 < B:
                    gru(0, g + 2)
                gru_out(g)
            pe.wait_ge(w2_in, 16 * 3 * E)
            pe.wait_ge(gruT_added, B)
            pe.wait_ge(dest_ready, 3)
            ffn(1)

        @block.scalar
        def _(act):
            fn = nc.scalar.activation
            for to, src in SMALL:
                act.dma_start(to[:], src).then_inc(small_in, 16)
            for to, src in BCAST:
                act.dma_start(to[:], src.partition_broadcast(P)).then_inc(small_in, 16)

            def normalise(l, t):
                fn(xn[:, t * ROW:t * ROW + D], x[:, t * D:(t + 1) * D], ACT.Identity, bias=ln[:, 2 * NT + t:2 * NT + t + 1],
                   scale=ln[:, NT + t:NT + t + 1]).then_inc(xn_act, 1)

            def exponentials(u):
                act.wait_ge(qkv_biased, u + 1)
                if u - NEX < FEAT_POOL:
                    after(act, feat_ready, u - NEX + 1)
                else:
                    act.wait_ge(feat_dve, u - NEX - FEAT_POOL + 1)
                qk = big[:, 2 * u * 3 * D:(2 * u + 2) * 3 * D].rearrange("p (t c) -> p t c", t=2)[:, :, 0:2 * D]
                fn(ex[u % NEX].rearrange("p (t c) -> p t c", t=2), qk, ACT.Exp).then_inc(feat_exp, 1)

            def tokens(l):
                def root(k):
                    act.wait_ge(var_ready, (LOADS + 1) * l + k + 1)
                    c8 = slice(3 * NT + k * TPL, 3 * NT + (k + 1) * TPL)
                    d8 = slice(4 * NT + k * TPL, 4 * NT + (k + 1) * TPL)
                    fn(ln[:, d8], ln[:, c8], ACT.Sqrt).then_inc(sqrt_ready, 1)

                def normalise_group(k):
                    act.wait_ge(rstd_ready, (LOADS + 1) * l + k + 1)
                    for t in range(k * TPL + 1, (k + 1) * TPL, 2):
                        normalise(l, t)

                def evict_xT(g):
                    act.wait_ge(xT_psum, l * B + g + 1)
                    fn(xnT[:, g * S:(g + 1) * S], bank[g % 2], ACT.Copy).then_inc(xT_ready, 1)

                def evict_projection(g):
                    act.wait_ge(proj_psum, g + 1)
                    after(act, proj_read, g - 1)
                    at = (2 + 2 * (g % 2)) * 512
                    pj = ps[:, at:at + 1024].rearrange("p (j c) -> p j c", j=TPS)
                    fn(sq[g % 2].rearrange("p (j c) -> p j c", j=TPS), pj[:, :, 0:D], ACT.Square)
                    fn(lg[:, g * TPS * E:(g + 1) * TPS * E].rearrange("p (j e) -> p j e", j=TPS),
                       pj[:, :, D:D + E], ACT.Copy).then_inc(proj_ready, 1)

                def evict_sequence(g):
                    evict_xT(g)
                    if l == 0 and g >= LAG:
                        exponentials(g - LAG)
                    if l == 1 and g:
                        evict_projection(g - 1)

                root(0)
                root(1)
                if l:
                    for part_listed in listed[0]:
                        act.wait_ge(part_listed, 16 * HALF)
                for k in range(LOADS):
                    normalise_group(k)
                    if l == 0 and k == LOADS - 1:
                        act.wait_ge(sim_sq, 1)
                        fn(simn[:, 1:2], simn[:, 0:1], ACT.Sqrt).then_inc(sim_root, 1)
                    if k:
                        evict_sequence(2 * k - 2)
                    if k + 2 < LOADS:
                        root(k + 2)
                    if k:
                        evict_sequence(2 * k - 1)
                for g in (B - 2, B - 1):
                    evict_sequence(g)
                if l:
                    evict_projection(B - 1)

            def gap_exps(l):
                act.wait_ge(gap_ready, l + 1)
                fn(rs[5][:], rs[4][:], ACT.Exp).then_inc(gap_exp, 1)

            act.wait_ge(var_ready, 1)
            tokens(0)
            for u in range(B - LAG, NT // 2):
                exponentials(u)
                if u == B + 1:
                    gap_exps(0)

            def evict_aT(g):
                act.wait_ge(aT_psum, g + 1)
                fn(aT, bank[4], ACT.Copy).then_inc(aT_ready, 1)

            def evict_o(g):
                act.wait_ge(o_psum, g + 1)
                fn(attn_o[:, g * S:(g + 1) * S], bank[4], ACT.Copy).then_inc(o_ready, 1)

            for g in range(B):
                if g:
                    evict_aT(g - 1)
                    evict_o(g - 1)
                act.wait_ge(qT_psum, g + 1)
                fn(qT[g % 2], bank[4], ACT.Copy).then_inc(qT_ready, 1)

            def ffn(l):
                first = l * NBLK

                def evict_x(n):
                    act.wait_ge(xgT_psum, n + 1)
                    after(act, gate_psum if l else up_psum, n - NXT + 1)
                    fn(xgT[n % NXT], bank[6][:, (n % NXT) * P:(n % NXT + 1) * P], ACT.Copy).then_inc(xgT_ready, 1)

                def evict_h(n):
                    act.wait_ge(hT_psum, n + 1)
                    after(act, y_psum, n - 1)
                    fn(hT[n % 2], bank[5], ACT.Copy).then_inc(hT_ready, 1)

                fn(idle[:], idle[:], ACT.Gelu)
                evict_x(first)
                evict_x(first + 1)
                for b in range(NBLK):
                    n = first + b
                    if l == 0:
                        act.wait_ge(gate_psum, n + 1)
                        after(act, h_ready, n - 1)
                        fn(fa[n % 2], bank[n % 2], ACT.Gelu).then_inc(act_ready, 1)
                        if b == B + 1:
                            act.wait_ge(var_ready, LOADS + 1)
                            fn(ln[:, 4 * NT:5 * NT], ln[:, 3 * NT:4 * NT], ACT.Sqrt).then_inc(sqrt_ready, 1)
                        if O_FROM <= b < O_FROM + NT:
                            t0 = b - O_FROM
                            if t0 == 0:
                                act.wait_ge(rstd_ready, LOADS + 1)
                            fn(attn_o[:, t0 * D:(t0 + 1) * D], attn_o[:, t0 * D:(t0 + 1) * D], ACT.Identity,
                               bias=ln[:, 2 * NT + t0:2 * NT + t0 + 1], scale=ln[:, NT + t0:NT + t0 + 1]).then_inc(o_normed, 1)
                    else:
                        act.wait_ge(pre_ready, b + 1)
                        after(act, hT_psum, n - 1)
                        fn(fh[n % 2], fa[n % 2], ACT.Gelu).then_inc(h_ready, 1)
                    if b + 2 < NBLK:
                        evict_x(n + 2)
                    if l == 0 and b < 2:
                        (evict_aT, evict_o)[b](B - 1)
                    if l and b:
                        evict_h(n - 1)
                if l:
                    evict_h(first + NBLK - 1)

            ffn(0)
            tokens(1)
            act.wait_ge(norms_ready, 1)
            fn(rs[2][:], rs[0][:], ACT.Sqrt).then_inc(sqrt_ready, 1)
            gap_exps(1)
            for n, (l, g) in enumerate(order):
                act.wait_ge(gru_psum, n + 1)
                s = g % 2
                last = max([k for k in range(n) if order[k][1] % 2 == s], default=-1)
                after(act, gru_scan, last + 1)
                fn(ga[s], bank[2 * l], ACT.Sigmoid, bias=bzh2[:, l:l + 1], scale=-1.0)
                fn(gz[s], bank[2 * l], ACT.Sigmoid, bias=bzh[:, l:l + 1])
                fn(gs[s], bank[2 * l + 1], ACT.Sigmoid, bias=bzh[:, 2 + l:3 + l]).then_inc(gru_act, 1)
            ffn(1)

        @block.vector
        def _(dve):
            v = nc.vector
            c = Chain(dve, dve_step)

            def three(a, n=E):
                return a.rearrange("p (t e) -> p t e", e=n)

            def variances(stats, k0, k1):
                st6 = stats[:, k0 * 6:k1 * 6].rearrange("p (t k) -> p t k", k=6)
                mean, var, a, b2, m2 = (ln[:, k * NT + k0:k * NT + k1] for k in (0, 3, 5, 6, 7))
                c.add(v.tensor_tensor(out=a, in0=st6[:, :, 1], in1=st6[:, :, 4], op=ALU.add))
                c.add(v.tensor_tensor(out=b2, in0=st6[:, :, 1], in1=st6[:, :, 4], op=ALU.subtract))
                c.link(v.tensor_tensor(out=m2, in0=st6[:, :, 2], in1=st6[:, :, 5], op=ALU.add))
                c.add(v.tensor_scalar(mean, a, 0.5, None, ALU.mult))
                c.link(v.tensor_tensor(out=b2, in0=b2, in1=b2, op=ALU.mult))
                c.link(v.scalar_tensor_tensor(out=m2, in0=b2, scalar=D / 4.0, in1=m2, op0=ALU.mult, op1=ALU.add))
                v.tensor_scalar(var, m2, 1.0 / D, LN_EPS, ALU.mult, ALU.add).then_inc(var_ready, 1)

            def inverse_root(r, root, value, t):
                c.link(v.reciprocal(r, root))
                c.link(v.tensor_tensor(out=t, in0=r, in1=r, op=ALU.mult))
                c.link(v.tensor_tensor(out=t, in0=t, in1=value, op=ALU.mult))
                c.link(v.tensor_scalar(t, t, -0.5, 1.5, ALU.mult, ALU.add))
                c.link(v.tensor_tensor(out=r, in0=r, in1=t, op=ALU.mult))

            def rstds(k0, k1):
                mean, rstd, shift, var, root, t = (ln[:, k * NT + k0:k * NT + k1] for k in (0, 1, 2, 3, 4, 5))
                inverse_root(rstd, root, var, t)
                v.scalar_tensor_tensor(out=shift, in0=mean, scalar=-1.0, in1=rstd, op0=ALU.mult, op1=ALU.mult)\
                    .then_inc(rstd_ready, 1)

            def moments(k):
                for t in range(k * TPL, (k + 1) * TPL):
                    c.add(v.bn_stats(st[:, t * 6:(t + 1) * 6], x[:, t * D:(t + 1) * D]))
                c.wait()
                variances(st, k * TPL, (k + 1) * TPL)

            def scales(l, k):
                dve.wait_ge(sqrt_ready, (LOADS + 1) * l + k + 1)
                rstds(k * TPL, (k + 1) * TPL)
                if k >= POOL_GROUPS:
                    dve.wait_ge(rstd_ready, (LOADS + 1) * l + k + 1)
                    for t in range(k * TPL, (k + 1) * TPL, 2):
                        v.tensor_scalar(xn[:, t * ROW:t * ROW + D], x[:, t * D:(t + 1) * D], ln[:, t:t + 1],
                                        ln[:, NT + t:NT + t + 1], ALU.subtract, ALU.mult).then_inc(xn_dve, 1)

            def route(l):
                eq_, cand, oh1, L2, oh2, tot, scan, dest = rt

                def per_tile(a):
                    return a[:].unsqueeze(2).to_broadcast([P, NT, E])

                revb = rev[:].unsqueeze(1).to_broadcast([P, NT, E])
                for scores, best, oh, r in ((lg[:], rs[0], oh1, rs[1]), (L2, rs[2], oh2, rs[3])):
                    yield v.tensor_reduce(out=best[:], in_=three(scores), axis=AX.X, op=ALU.max)
                    yield v.tensor_tensor(out=three(eq_), in0=three(scores), in1=per_tile(best), op=ALU.is_equal)
                    yield v.tensor_tensor(out=three(cand), in0=three(eq_), in1=revb, op=ALU.mult)
                    yield v.tensor_reduce(out=r[:], in_=three(cand), axis=AX.X, op=ALU.max)
                    yield v.tensor_tensor(out=three(oh), in0=three(cand), in1=per_tile(r), op=ALU.is_equal)
                    if oh is oh1:
                        yield v.scalar_tensor_tensor(out=L2, in0=oh1, scalar=-BIG, in1=lg[:], op0=ALU.mult, op1=ALU.add)
                v.tensor_tensor(out=m16[:].rearrange("p (e t) -> p t e", e=E), in0=three(oh1), in1=three(oh2),
                                op=ALU.add).then_inc(picks_ready, 1)
                v.tensor_tensor(out=rs[4][:], in0=rs[2][:], in1=rs[0][:], op=ALU.subtract).then_inc(gap_ready, 1)
                dve.wait_ge(ranks_psum, l + 1)
                yield v.tensor_copy(tot, bank[5][:, 256:512])
                yield v.tensor_tensor_scan(out=scan, data0=ones[:], data1=tot, initial=0.0, op0=ALU.mult, op1=ALU.add)
                ends = scan.rearrange("p (e t) -> p e t", e=E)
                yield v.tensor_copy(r9[:, 1:E + 1], ends[:, :, NT - 1])
                yield v.tensor_tensor(out=r8[0][:], in0=r9[:, 1:E + 1], in1=r9[:, 0:E], op=ALU.subtract)
                yield v.tensor_scalar(r8i[0][:], r8[0][:], float(P - 1), None, ALU.add)
                sh = P.bit_length() - 1
                yield v.tensor_scalar(r8i[1][:], r8i[0][:], sh, sh, ALU.logical_shift_right, ALU.logical_shift_left)
                yield v.tensor_copy(r8[1][:], r8i[1][:])
                yield v.tensor_tensor_scan(out=r8[2][:], data0=ones[:, 0:E], data1=r8[1][:], initial=0.0,
                                            op0=ALU.mult, op1=ALU.add)
                yield v.tensor_tensor(out=r8[3][:], in0=r8[2][:], in1=r8[1][:], op=ALU.subtract)
                yield v.tensor_tensor(out=r8[4][:], in0=r8[3][:], in1=r9[:, 0:E], op=ALU.subtract)
                dve.wait_ge(gap_exp, l + 1)
                yield v.tensor_scalar(rs[6][:], rs[5][:], 1.0, None, ALU.add)
                yield v.reciprocal(wgt[0][:], rs[6][:])
                v.tensor_tensor(out=wgt[1][:], in0=rs[5][:], in1=wgt[0][:], op=ALU.mult).then_inc(weights_ready, 1)
                yield v.tensor_tensor(out=scan, in0=scan, in1=tot, op=ALU.subtract)
                yield v.tensor_tensor(out=scan, in0=scan, in1=bank[5][:, 0:256], op=ALU.add)
                yield v.tensor_tensor(out=dest.rearrange("p (e t) -> p e t", e=E), in0=ends,
                                       in1=r8[4][:].unsqueeze(2).to_broadcast([P, E, NT]), op=ALU.add)
                for k, oh in enumerate((oh1, oh2)):
                    yield v.tensor_tensor(out=three(cand), in0=three(oh),
                                           in1=dest.rearrange("p (e t) -> p t e", e=E), op=ALU.mult)
                    yield v.tensor_reduce(out=rs[7][:], in_=three(cand), axis=AX.X, op=ALU.add)
                    v.tensor_copy(dst[l][k][:], rs[7][:]).then_inc(dest_ready, 1)
                cmpb = sto[0:1, :]
                yield v.tensor_tensor(out=three(cmpb), in0=blk_start[:].unsqueeze(2).to_broadcast([1, NBLK, E]),
                                       in1=r8[2][0:1, :].unsqueeze(1).to_broadcast([1, NBLK, E]), op=ALU.is_ge)
                yield v.tensor_reduce(out=bexf[:], in_=three(cmpb), axis=AX.X, op=ALU.add)
                v.tensor_scalar(bex[l][:], bexf[:], float(E - 1), None, ALU.min).then_inc(blocks_ready, 1)

            def advance(steps, n=1):
                for _ in range(n):
                    c.wait()
                    ins = next(steps, None)
                    if ins is None:
                        return
                    c.add(ins)

            for k in range(LOADS):
                dve.wait_ge(x_in[k], 16)
                moments(k)
                if k:
                    scales(0, k - 1)
            scales(0, LOADS - 1)
            dve.wait_ge(small_in, NSMALL)
            c.add(v.tensor_scalar(bzh2[:, 0:2], bzh[:, 0:2], -1.0, None, ALU.mult))
            c.add(v.tensor_scalar(bzh2[:, 2:4], bzh[:, 2:4], 0.5, None, ALU.add))
            c.add(v.reciprocal(rtemp[:], tempb[:]))
            simsq = tmp[0:E, S:S + D]
            c.link(v.tensor_tensor(out=simsq, in0=sim[:], in1=sim[:], op=ALU.mult))
            c.link(v.tensor_reduce(out=simn[:, 3:4], in_=simsq, axis=AX.X, op=ALU.add))
            v.tensor_scalar(simn[:, 0:1], simn[:, 3:4], NORM_EPS * NORM_EPS, None, ALU.max).then_inc(sim_sq, 1)


            def bias(u):
                dve.wait_ge(qkv_psum, u + 1)
                pair = QKV_BANKS[u % 2]
                v.tensor_tensor(out=big[:, 2 * u * 3 * D:(2 * u + 2) * 3 * D].rearrange("p (t c) -> p t c", t=2),
                                in0=ps[:, pair * 512:(pair + 2) * 512].rearrange("p (t c) -> p t c", t=2)[:, :, 0:3 * D],
                                in1=bqkvb[:].unsqueeze(1).to_broadcast([P, 2, 3 * D]), op=ALU.add).then_inc(qkv_biased, 1)

            steps = route(0)
            bias(0)
            for u in range(NT // 2):
                if u + 1 < NT // 2:
                    bias(u + 1)
                if u == B - 1:
                    dve.wait_ge(sim_root, 1)
                    inverse_root(simn[:, 2:3], simn[:, 1:2], simn[:, 0:1], simn[:, 3:4])
                    v.tensor_scalar(sim[:], sim[:], simn[:, 2:3], None, ALU.mult).then_inc(simn_ready, 1)
                if u == B:
                    dve.wait_ge(scored, B)
                    dve.wait_ge(consts_ready, 1)
                    c.add(v.tensor_copy(lg[:], bank[4][:, 0:NT * E]))
                if u >= B:
                    advance(steps)
                qk = big[:, 2 * u * 3 * D:(2 * u + 2) * 3 * D].rearrange("p (t c) -> p t c", t=2)[:, :, 0:2 * D]
                dve.wait_ge(feat_exp, u + 1)
                ins = v.tensor_scalar(qk, qk, FEAT_EPS, FEAT_EPS, ALU.add, ALU.max).then_inc(feat_max, 1)
                if u >= B:
                    advance(steps, 3)
                if u >= FEAT_POOL:
                    dve.wait_ge(feat_max, u + 1)
                    v.scalar_tensor_tensor(out=qk, in0=ex[u % NEX].rearrange("p (t c) -> p t c", t=2), scalar=1.0, in1=qk,
                                           op0=ALU.min, op1=ALU.add).then_inc(feat_dve, 1)
                if u >= B:
                    advance(steps, 2)
                if u == B + 3:
                    dve.wait_ge(simT_psum, 1)
                    v.tensor_copy(simT[:], bank[4][:, 0:E])
                    v.tensor_copy(wpT[:], bank[4][:, P:2 * P]).then_inc(simT_ready, 1)
                if u == B + 4:
                    dve.wait_ge(simT_psum, 2)
                    v.tensor_copy(wps[:, D:D + E], bank[4][:, 0:E]).then_inc(simT_ready, 1)
                if u >= NT // 2 - 2:
                    t = u - (NT // 2 - 2)
                    dve.wait_ge(feat_ready, 1)
                    outer(v, t).then_inc(kvx_ready, 1)
            advance(steps, ROUTE_STEPS)
            dve.wait_ge(feat_ready, FEAT_POOL)
            dve.wait_ge(feat_dve, NT // 2 - FEAT_POOL)

            def query(t):
                pair = 2 * (t % 2)
                dve.wait_ge(tri_psum, t + 1)
                v.tensor_tensor(out=pr[t % 2].rearrange("p (h f e) -> p h f e", h=H, f=HE),
                                in0=ps[:, pair * 512:(pair + 2) * 512].rearrange("p (h f e) -> p h f e", h=H, f=HE),
                                in1=heads(qkv(t, 0)).unsqueeze(2).to_broadcast([P, H, HE, HE]),
                                op=ALU.mult).then_inc(prod_ready, 1)

            def reduce(t):
                g, j = t // TPS, t % TPS
                dve.wait_ge(prod_ready, t + 1)
                c.add(v.tensor_reduce(out=red[g % 2][:, j * D:(j + 1) * D], in_=heads(pr[t % 2]), axis=AX.X, op=ALU.add))

            def mask(t):
                g, j = t // TPS, t % TPS
                dve.wait_ge(state_psum, g * (TPS - 1) + j + 1)
                v.tensor_tensor(out=stt[j], in0=bank[5][:, 0:P + H], in1=smask[:], op=ALU.mult).then_inc(state_ready, 1)

            def k_sums(g):
                dve.wait_ge(ksum_psum, (g + 1) * TPS)
                qs = big[:, 3 * g * S:3 * (g + 1) * S].rearrange("p (t c) -> p t c", t=TPS)[:, :, 0:D]
                v.tensor_tensor(out=kq.rearrange("p (t c) -> p t c", t=TPS), in0=bank[6].rearrange("p (t c) -> p t c", t=TPS),
                                in1=qs, op=ALU.mult).then_inc(kq_ready, 1)
                dve.wait_ge(kq_ready, g + 1)
                c.add(v.tensor_reduce(out=dred, in_=heads(kq), axis=AX.X, op=ALU.add))

            def divide(g):
                r = red[g % 2]
                dve.wait_ge(inter_psum, g + 1)
                c.wait()
                c.add(v.tensor_tensor(out=r[:, D:], in0=r[:, D:], in1=bank[7][:, D:], op=ALU.add))
                v.tensor_tensor(out=dred[:, H:], in0=dred[:, H:], in1=bank[7][:, H:TPS * H], op=ALU.add)\
                    .then_inc(sums_ready, 1)
                dve.wait_ge(sums_ready, g + 1)
                c.link(v.tensor_scalar(rden, dred, FEAT_EPS * HE ** 0.5, None, ALU.add))
                c.link(v.reciprocal(rden, rden))
                after(dve, aT_psum, g)
                v.tensor_tensor(out=heads(att), in0=heads(r), in1=rden.unsqueeze(2).to_broadcast([P, TPS * H, HE]),
                                op=ALU.mult).then_inc(att_ready, 1)

            def stats(g):
                dve.wait_ge(o_ready, g + 1)
                for t in range(g * TPS, (g + 1) * TPS):
                    c.add(v.bn_stats(sto[:, t * 6:(t + 1) * 6], attn_o[:, t * D:(t + 1) * D]))

            outer(v, 2).then_inc(kvx_ready, 1)
            for t in range(NT):
                g, j = t // TPS, t % TPS
                query(t)
                if 3 <= t + 2 < NT and not by_pool(t + 2):
                    outer(v, t + 2).then_inc(kvx_ready, 1)
                reduce(t)
                if j == 0 and g:
                    divide(g - 1)
                if j < TPS - 1:
                    mask(t)
                else:
                    k_sums(g)
            divide(B - 1)
            def ffn(l):
                first = l * NBLK
                e = {}

                def load_expert(n):
                    e[n] = dve.value_load(bex[l][0:1, n - first:n - first + 1], min_val=0, max_val=E - 1)

                def hidden(n):
                    if l == 0:
                        dve.wait_ge(up_psum, n + 1)
                        dve.wait_ge(act_ready, n + 1)
                        after(dve, hT_psum, n - 1)
                        v.tensor_tensor(out=fh[n % 2], in0=bank[2 + n % 2], in1=fa[n % 2], op=ALU.mult)\
                            .then_inc(h_ready, 1)
                    else:
                        dve.wait_ge(gate_psum, n + 1)
                        after(dve, h_ready, n - 1)
                        v.tensor_tensor(out=fa[n % 2], in0=bank[n % 2], in1=b1b[:, bass.ds(e[n] * F, F)], op=ALU.add)\
                            .then_inc(pre_ready, 1)

                def evict_h(n):
                    dve.wait_ge(hT_psum, n + 1)
                    after(dve, y_psum, n - 1)
                    v.tensor_copy(hT[n % 2], bank[5]).then_inc(hT_ready, 1)

                def evict_y(n):
                    dve.wait_ge(y_psum, n + 1)
                    if n >= NYB:
                        dve.wait_ge(y_out[n % NYB], 16 * (n // NYB))
                    src = bank[7][:, (n % 2) * P:(n % 2 + 1) * P]
                    if l:
                        c.link(v.tensor_tensor(out=yb[n % NYB], in0=src, in1=b2b[:, bass.ds(e.pop(n) * D, D)], op=ALU.add))
                        src = yb[n % NYB]
                    v.tensor_scalar(yb[n % NYB], src, xg[n % NXG][:, WGT:WGT + 1], None, ALU.mult).then_inc(y_ready, 1)

                if l:
                    dve.wait_ge(blocks_ready, 2)
                    load_expert(first)
                for b in range(NBLK + 2):
                    n = first + b
                    if b < NBLK:
                        hidden(n)
                    if b >= 2:
                        evict_y(n - 2)
                    if l == 0 and 1 <= b <= NBLK:
                        evict_h(n - 1)
                    if l == 0 and b < B:
                        stats(b)
                    if l == 0 and b == B:
                        c.wait()
                        variances(sto, 0, NT)
                    if l == 0 and b == B + 2:
                        dve.wait_ge(sqrt_ready, LOADS + 1)
                        rstds(0, NT)
                    if l and b + 1 < NBLK:
                        load_expert(n + 1)

            ffn(0)

            def add_results(l, k):
                dve.wait_ge(y_summed, l * LOADS + k + 1)
                w = NT * D // (LOADS, STORES)[l]
                xk = x[:, k * w:(k + 1) * w]
                return v.tensor_tensor(out=xk, in0=xk, in1=y[0][:, k * w:(k + 1) * w], op=ALU.add)

            def square_sums(g):
                dve.wait_ge(proj_ready, g + 1)
                v.tensor_reduce(out=rs[7][:, g * TPS:(g + 1) * TPS], in_=heads(sq[g % 2], D), axis=AX.X, op=ALU.add)\
                    .then_inc(proj_read, 1)

            dve.wait_ge(attn_added, B)
            for k in range(LOADS):
                add_results(0, k).then_inc(x_added, 1)
                dve.wait_ge(x_added, k + 1)
                moments(k)
                if k == 1:
                    for part_listed in listed[0]:
                        dve.wait_ge(part_listed, 16 * HALF)
                if k:
                    scales(1, k - 1)
            scales(1, LOADS - 1)
            for g in range(B):
                square_sums(g)
            dve.wait_ge(proj_read, B)
            v.tensor_scalar(rs[0][:], rs[7][:], NORM_EPS * NORM_EPS, None, ALU.max).then_inc(norms_ready, 1)
            dve.wait_ge(norms_ready, 1)
            dve.wait_ge(sqrt_ready, 2 * LOADS + 2)
            inverse_root(rs[1][:], rs[2][:], rs[0][:], rs[3][:])
            c.link(v.tensor_scalar(rs[3][:], rs[1][:], rtemp[:], None, ALU.mult))
            c.link(v.tensor_tensor(out=three(lg[:]), in0=three(lg[:]),
                                   in1=rs[3][:].unsqueeze(2).to_broadcast([P, NT, E]), op=ALU.mult))
            advance(route(1), ROUTE_STEPS)

            def gru_add(g):
                dve.wait_ge(gruT_psum, g + 1)
                v.tensor_tensor(out=x[:, g * S:(g + 1) * S], in0=x[:, g * S:(g + 1) * S], in1=bank[7], op=ALU.add)\
                    .then_inc(gruT_added, 1)

            for n, (l, g) in enumerate(order):
                s = g % 2
                h = (gh1, gh2)[l][s]
                dve.wait_ge(gru_act, n + 1)
                c.link(v.scalar_tensor_tensor(out=gs[s], in0=bank[2 * l + 1], scalar=bzh2[:, 2 + l:3 + l], in1=gs[s],
                                              op0=ALU.add, op1=ALU.max))
                c.link(v.tensor_tensor(out=gz[s], in0=gz[s], in1=gs[s], op=ALU.mult))
                if l == 1:
                    after(dve, gruT_psum, g - 1)
                else:
                    after(dve, gru_psum, order.index((1, g - 2)) + 1 if g >= 2 else 0)
                v.tensor_tensor_scan(out=h, data0=ga[s], data1=gz[s], initial=0.5, op0=ALU.mult, op1=ALU.add)\
                    .then_inc(gru_scan, 1)
                if l == 1 and g:
                    gru_add(g - 1)
            gru_add(B - 1)
            dve.wait_ge(w2_in, 16 * 3 * E)
            ffn(1)
            for k in range(STORES):
                add_results(1, k).then_inc(out_ready, 1)


def kernel(**inputs):
    import numpy as _np
    import concourse.bacc as _bacc
    from concourse import mybir as _mybir
    from concourse.bass_utils import run_bass_kernel_spmd as _run

    a = {k: _np.asarray(v) for k, v in inputs.items()}
    wqkv = a["L0_attn_Wqkv"]
    laid = {
        "x": a["L0_attn_x"],
        "wqkv": wqkv.T,
        "bqkv": a["L0_attn_bqkv"],
        "wout": a["L0_attn_Wout"].T,
        "bout": a["L0_attn_bout"].reshape(1, 128), "gamma": a["L0_attn_gamma"], "beta": a["L0_attn_beta"],
        "gatew": a["L0_ffn_gate_w"].T,
        "gu": a["L0_ffn_gate_up_w"].transpose(2, 0, 1).reshape(128, -1),
        "dw": a["L0_ffn_down_w"].reshape(8, 128, 4, 128).transpose(3, 0, 2, 1).reshape(128, -1),
        "wz": a["L1_attn_Wz"].transpose(2, 0, 1).reshape(128, -1), "bz": a["L1_attn_bz"].T,
        "wh": a["L1_attn_Wh"].transpose(2, 0, 1).reshape(128, -1), "bh": a["L1_attn_bh"].T,
        "wp": a["L1_ffn_Wp"].T, "sim": a["L1_ffn_sim_matrix"], "temp": a["L1_ffn_temperature"].reshape(1),
        "w1": a["L1_ffn_W1"].transpose(1, 0, 2).reshape(128, -1), "b1": a["L1_ffn_b1"].reshape(-1),
        "w2": a["L1_ffn_W2"].reshape(8, 4, 128, 128).transpose(2, 0, 1, 3).reshape(128, -1),
        "b2": a["L1_ffn_b2"].reshape(-1),
    }
    nc = _bacc.Bacc("TRN2", target_bir_lowering=False, num_devices=1)
    arrays, args = {}, []
    for name, v in laid.items():
        v = _np.ascontiguousarray(v)
        arrays[f"in_{name}"] = v
        args.append(nc.dram_tensor(f"in_{name}", v.shape, _mybir.dt.from_np(v.dtype), kind="ExternalInput").ap())
    f32 = _mybir.dt.float32
    for l in range(2):
        args.append(nc.dram_tensor(f"sorted_tokens{l}", (NBLK * P, ROW), f32, kind="Internal").ap())
    args.append(nc.dram_tensor("results", ((2 * NT + NBLK) * P, D), f32, kind="Internal").ap())
    args.append(nc.dram_tensor("out", (B, S, D), f32, kind="ExternalOutput").ap())
    build(nc, *args)
    return _run(nc, [arrays], core_ids=[0]).results[0]["out"]
```
